# Optimizing a Trainium2 kernel written in Bass

```python
import numpy as np
import jax
import jax.numpy as jnp

def _softmax(x, axis=-1):
    return jax.nn.softmax(x, axis=axis)

def _gelu(x):
    return jax.nn.gelu(x, approximate=True)

def _silu(x):
    return jax.nn.silu(x)

def _sigmoid(x):
    return jax.nn.sigmoid(x)

def _layernorm(x, axis=-1, eps=1e-05):
    m = jnp.mean(x, axis=axis, keepdims=True)
    v = jnp.var(x, axis=axis, keepdims=True)
    return (x - m) / jnp.sqrt(v + eps)

def _scatter_add(tgt, idx, src, axis=0):
    return tgt.at[idx].add(src)

def _segment_sum(src, seg, n):
    return jax.ops.segment_sum(src, seg, n)
kernel_name = 'mk_prb_d4_jaxref_r8_f64f32'

def setup_inputs(seed: int=0):
    np.random.seed(seed)
    _w = jnp.asarray

    def _L0_attn_setup():
        import jax, jax.numpy as jnp
        import numpy as np
        EPS = 1e-08

        def rms_norm(x, scale):
            d = x.shape[-1]
            norm = jnp.linalg.norm(x, ord=2, axis=-1, keepdims=True)
            rms = norm * d ** (-0.5)
            return scale * (x / (rms + EPS))
        key = jax.random.key(seed)
        ks = jax.random.split(key, 4)
        B, N, C, H = (2, 256, 128, 16)
        hd = C // H
        x = jax.random.normal(ks[0], (B, N, C), dtype=jnp.float32)
        Wqkv = jax.random.normal(ks[1], (C, 3 * C), dtype=jnp.float32) * C ** (-0.5)
        Wproj = jax.random.normal(ks[2], (C, C), dtype=jnp.float32) * C ** (-0.5)
        bproj = jnp.zeros((C,), dtype=jnp.float32)
        q_scale = jnp.ones((hd,), dtype=jnp.float32)
        k_scale = jnp.ones((hd,), dtype=jnp.float32)
        return {'x': x, 'Wqkv': Wqkv, 'Wproj': Wproj, 'bproj': bproj, 'q_scale': q_scale, 'k_scale': k_scale}
    _L0_attn_in = _L0_attn_setup()

    def _L0_ffn_setup():
        import jax, jax.numpy as jnp
        import numpy as np
        NUM_TRUE = 8
        NUM_NULL = 2
        NUM_EXPERTS = NUM_TRUE + NUM_NULL
        TOP_K = 2
        key = jax.random.key(seed)
        k0, k1, k2 = jax.random.split(key, 3)
        B, S, D = (4, 256, 128)
        inputs = jax.random.normal(k0, (B, S, D), dtype=jnp.float32)
        gate_w = jax.random.normal(k1, (NUM_EXPERTS, D), dtype=jnp.float32) * 0.02
        gate_b = jnp.zeros((NUM_EXPERTS,), dtype=jnp.float32)
        expert_w = jax.random.normal(k2, (NUM_TRUE, D, D), dtype=jnp.float32) * 0.02
        expert_b = jnp.zeros((NUM_TRUE, D), dtype=jnp.float32)
        return {'inputs': inputs, 'gate_w': gate_w, 'gate_b': gate_b, 'expert_w': expert_w, 'expert_b': expert_b}
    _L0_ffn_in = _L0_ffn_setup()

    def _L1_attn_setup():
        import jax, jax.numpy as jnp
        import numpy as np
        B, T, D, DS = (8, 512, 128, 64)
        key = jax.random.key(seed)
        ks = jax.random.split(key, 9)
        s = 0.02
        return {'x': jax.random.normal(ks[0], (B, T, D), dtype=jnp.float32), 'Wq': jax.random.normal(ks[1], (DS, D), dtype=jnp.float32) * s, 'bq': jnp.zeros((DS,), dtype=jnp.float32), 'Wk': jax.random.normal(ks[2], (DS, D), dtype=jnp.float32) * s, 'bk': jnp.zeros((DS,), dtype=jnp.float32), 'Wv': jax.random.normal(ks[3], (DS, D), dtype=jnp.float32) * s, 'bv': jnp.zeros((DS,), dtype=jnp.float32), 'decay': jnp.full((DS,), 0.95, dtype=jnp.float32), 'Wo': jax.random.normal(ks[4], (D, DS), dtype=jnp.float32) * s, 'bo': jnp.zeros((D,), dtype=jnp.float32)}
    _L1_attn_in = _L1_attn_setup()

    def _L1_ffn_setup():
        import math
        import jax, jax.numpy as jnp
        import numpy as np
        D_MODEL = 128
        NUM_EXPERTS = 8
        D_FF_EXPERT = max(64, int(D_MODEL * 4 * 0.25))
        THRESHOLD = 0.9
        CAP_FACTOR = 1.0
        INIT_STD = 0.02

        def _xmoe_route(probs):
            N, E = probs.shape
            order = jnp.argsort(-probs, axis=-1)
            p_sorted = jnp.take_along_axis(probs, order, axis=-1)
            csum = jnp.cumsum(p_sorted, axis=-1)
            reached = (csum >= THRESHOLD).at[:, -1].set(True)
            k_idx = jnp.argmax(reached, axis=-1)
            select_prefix = jnp.arange(E)[None, :] <= k_idx[:, None]
            rows = jnp.arange(N)[:, None]
            assign_mask = jnp.zeros((N, E), dtype=bool).at[rows, order].set(select_prefix)
            rank = jnp.arange(1, E + 1, dtype=probs.dtype)[None, :]
            R_sorted = jnp.where(select_prefix, p_sorted - rank, jnp.full_like(p_sorted, -1000000000.0))
            R = jnp.zeros((N, E), dtype=probs.dtype).at[rows, order].set(R_sorted)
            capacity = int(math.ceil(N / E) * CAP_FACTOR)
            C = min(capacity, N)
            tok_order = jnp.argsort(-R, axis=0)
            topC = tok_order[:C, :]
            keep = jnp.zeros((N, E), dtype=bool).at[topC, jnp.arange(E)[None, :]].set(True)
            final_mask = assign_mask & keep
            return jnp.where(final_mask, probs, jnp.zeros_like(probs))
        key = jax.random.key(seed)
        k_x, k_g, k_w1, k_w2 = jax.random.split(key, 4)
        B, T = (4, 256)
        x = jax.random.normal(k_x, (B, T, D_MODEL), dtype=jnp.float32)
        bound = 1.0 / math.sqrt(D_MODEL)
        gate_w = jax.random.uniform(k_g, (NUM_EXPERTS, D_MODEL), minval=-bound, maxval=bound, dtype=jnp.float32)
        w1 = INIT_STD * jax.random.normal(k_w1, (NUM_EXPERTS, D_FF_EXPERT, D_MODEL), dtype=jnp.float32)
        w2 = INIT_STD * jax.random.normal(k_w2, (NUM_EXPERTS, D_MODEL, D_FF_EXPERT), dtype=jnp.float32)
        return {'x': x, 'gate_w': gate_w, 'w1': w1, 'w2': w2}
    _L1_ffn_in = _L1_ffn_setup()

    def _L2_attn_setup():
        import jax, jax.numpy as jnp
        import numpy as np
        B, N = (2, 256)
        H, R = (8, 64)
        IN_DIM, OUT_DIM = (64, 64)
        D = IN_DIM + OUT_DIM
        INIT = 1.0
        key = jax.random.key(seed)
        k1, k2, k3, k4 = jax.random.split(key, 4)
        x = jax.random.normal(k1, (B, N, D), dtype=jnp.float32)
        Wq = jax.random.normal(k2, (H * R, D), dtype=jnp.float32) * (INIT / np.sqrt(H * R * D))
        Wk = jax.random.normal(k3, (H * R, D), dtype=jnp.float32) * (INIT / np.sqrt(H * R * D))
        Wv = jax.random.normal(k4, (H * D, D), dtype=jnp.float32) * (INIT / np.sqrt(H * D * D))
        Wk = Wk.at[:, -1].set(0.0)
        rows = np.arange(1, H + 1) * D - 1
        Wv = Wv.at[rows, :IN_DIM].set(0.0)
        return {'x': x, 'Wq': Wq, 'Wk': Wk, 'Wv': Wv}
    _L2_attn_in = _L2_attn_setup()

    def _L2_ffn_setup():
        import jax, jax.numpy as jnp
        import numpy as np
        D_IN, D_HID = (128, 512)

        def _ternary(key, shape):
            return jax.random.randint(key, shape, -1, 2).astype(jnp.float32)

        def _tlin(x, w, s):
            return jnp.einsum('bsi,oi->bso', x, w) * s
        key = jax.random.key(seed)
        ks = jax.random.split(key, 12)
        inv = lambda fan: 1.0 / np.sqrt(fan).astype(np.float32)
        return {'x': jax.random.normal(ks[0], (4, 256, D_IN), dtype=jnp.float32), 'w1_w': _ternary(ks[1], (D_HID, D_IN)), 'w1_s': jax.random.uniform(ks[2], (D_HID,), dtype=jnp.float32) * inv(D_IN), 'w2_w': _ternary(ks[3], (D_HID, D_IN)), 'w2_s': jax.random.uniform(ks[4], (D_HID,), dtype=jnp.float32) * inv(D_IN), 'h1_w': _ternary(ks[5], (D_HID, D_HID)), 'h1_s': jax.random.uniform(ks[6], (D_HID,), dtype=jnp.float32) * inv(D_HID), 'h2_w': _ternary(ks[7], (D_HID, D_HID)), 'h2_s': jax.random.uniform(ks[8], (D_HID,), dtype=jnp.float32) * inv(D_HID), 'w3_w': _ternary(ks[9], (D_IN, D_HID)), 'w3_s': jax.random.uniform(ks[10], (D_IN,), dtype=jnp.float32) * inv(D_HID)}
    _L2_ffn_in = _L2_ffn_setup()

    def _L3_attn_setup():
        import jax, jax.numpy as jnp
        import numpy as np
        B, T, D, H, LORA = (4, 128, 128, 16, 64)
        HD = D // H
        BLOCK_ID, N_BLOCKS = (6, 12)

        def _ln(x, w, b, eps=1e-05):
            m = x.mean(-1, keepdims=True)
            v = ((x - m) ** 2).mean(-1, keepdims=True)
            return (x - m) * jax.lax.rsqrt(v + eps) * w + b

        def _lora(z, a, b, l):
            return l + jnp.tanh(z @ a.T) @ b.T

        def _reference_tuple_inner(x, xw, rW, kW, vW, gW, r_la, r_lb, r_ll, k_la, k_lb, k_ll, v_la, v_lb, v_ll, g_la, g_lb, g_ll, d_la, d_lb, d_ll, ln_w, ln_b, oW, init_state, u):
            b, t, d = x.shape
            h = init_state.shape[0]
            hd = d // h
            xx = jnp.concatenate([jnp.zeros_like(x[:, :1]), x[:, :-1]], axis=1)
            dx = xx - x
            lerpx = x + dx * xw
            r = (x + dx * _lora(lerpx, r_la, r_lb, r_ll)) @ rW.T
            k = (x + dx * _lora(lerpx, k_la, k_lb, k_ll)) @ kW.T
            v = (x + dx * _lora(lerpx, v_la, v_lb, v_ll)) @ vW.T
            g = (x + dx * _lora(lerpx, g_la, g_lb, g_ll)) @ gW.T
            w = jnp.exp(-jnp.exp(_lora(x + dx * _lora(lerpx, d_la, d_lb, d_ll), d_la, d_lb, d_ll)))
            split = lambda z: z.reshape(b, t, h, hd).transpose(1, 0, 2, 3)
            rs, ws, ks, vs = (split(r), split(w), split(k), split(v))
            uh = u.reshape(h, hd)
            st0 = jnp.broadcast_to(init_state, (b, h, hd, hd))

            def step(st, inp):
                rt, wt, kt, vt = inp
                kv = jnp.einsum('bhi,bhj->bhij', kt, vt)
                y = jnp.einsum('bhi,bhij->bhj', rt, st + uh[None, :, :, None] * kv)
                return (wt[..., None] * st + kv, y)
            st1, ys = jax.lax.scan(step, st0, (rs, ws, ks, vs))
            o = jax.nn.silu(g.reshape(b, t, h, hd)) * _ln(ys.transpose(1, 0, 2, 3), ln_w, ln_b)
            return (o.reshape(b, t, d) @ oW.T, st1)
        key = jax.random.key(seed)
        ks = iter(jax.random.split(key, 64))
        rn = lambda shape, s: jax.random.normal(next(ks), shape, jnp.float32) * s
        inp = {}
        inp['x'] = rn((B, T, D), 1.0)
        r1 = 1.0 - BLOCK_ID / N_BLOCKS
        i = np.arange(D)
        inp['xw'] = jnp.asarray(1.0 - (i / D) ** r1, jnp.float32)
        for nm in ('rW', 'kW', 'vW', 'gW'):
            inp[nm] = rn((D, D), 0.02)
        for p in ('r', 'k', 'v', 'g', 'd'):
            inp[p + '_la'] = rn((LORA, D), 0.001)
            inp[p + '_lb'] = rn((D, LORA), 0.001)
            inp[p + '_ll'] = rn((D,), 1.0)
        inp['ln_w'] = jnp.full((HD,), ((1 + BLOCK_ID) / N_BLOCKS) ** 0.7, jnp.float32)
        inp['ln_b'] = jnp.zeros((HD,), jnp.float32)
        inp['oW'] = rn((D, D), 0.02)
        inp['init_state'] = rn((H, HD, HD), 1.0)
        r0 = BLOCK_ID / (N_BLOCKS - 1)
        ih = i % HD
        inp['u'] = jnp.asarray(r0 * (1 - ih / (D - 1)) + np.remainder(0.1 * (ih + 1), 3.0), jnp.float32)
        return inp
    _L3_attn_in = _L3_attn_setup()

    def _L3_ffn_setup():
        import jax, jax.numpy as jnp
        import numpy as np
        EMB = 128
        FF = 4 * EMB

        def _ternary(w):
            scale = jnp.maximum(jnp.mean(jnp.abs(w)), 1e-08)
            w_t = jnp.clip(jnp.round(w / scale), -1.0, 1.0)
            return w + jax.lax.stop_gradient(w_t - w)
        key = jax.random.key(seed)
        kx, k1, k2, kb1, kb2 = jax.random.split(key, 5)
        x = jax.random.normal(kx, (4, 256, EMB), dtype=jnp.float32)
        lim1 = 1.0 / np.sqrt(EMB)
        lim2 = 1.0 / np.sqrt(FF)
        W1 = jax.random.uniform(k1, (FF, EMB), jnp.float32, -lim1, lim1)
        b1 = jax.random.uniform(kb1, (FF,), jnp.float32, -lim1, lim1)
        W2 = jax.random.uniform(k2, (EMB, FF), jnp.float32, -lim2, lim2)
        b2 = jax.random.uniform(kb2, (EMB,), jnp.float32, -lim2, lim2)
        return {'x': x, 'W1': W1, 'b1': b1, 'W2': W2, 'b2': b2}
    _L3_ffn_in = _L3_ffn_setup()
    _d = {'L0_attn_x': _L0_attn_in['x'], 'L0_attn_Wqkv': _L0_attn_in['Wqkv'], 'L0_attn_Wproj': _L0_attn_in['Wproj'], 'L0_attn_bproj': _L0_attn_in['bproj'], 'L0_attn_q_scale': _L0_attn_in['q_scale'], 'L0_attn_k_scale': _L0_attn_in['k_scale'], 'L0_ffn_gate_w': _L0_ffn_in['gate_w'], 'L0_ffn_gate_b': _L0_ffn_in['gate_b'], 'L0_ffn_expert_w': _L0_ffn_in['expert_w'], 'L0_ffn_expert_b': _L0_ffn_in['expert_b'], 'L1_attn_Wq': _L1_attn_in['Wq'], 'L1_attn_bq': _L1_attn_in['bq'], 'L1_attn_Wk': _L1_attn_in['Wk'], 'L1_attn_bk': _L1_attn_in['bk'], 'L1_attn_Wv': _L1_attn_in['Wv'], 'L1_attn_bv': _L1_attn_in['bv'], 'L1_attn_decay': _L1_attn_in['decay'], 'L1_attn_Wo': _L1_attn_in['Wo'], 'L1_attn_bo': _L1_attn_in['bo'], 'L1_ffn_gate_w': _L1_ffn_in['gate_w'], 'L1_ffn_w1': _L1_ffn_in['w1'], 'L1_ffn_w2': _L1_ffn_in['w2'], 'L2_attn_Wq': _L2_attn_in['Wq'], 'L2_attn_Wk': _L2_attn_in['Wk'], 'L2_attn_Wv': _L2_attn_in['Wv'], 'L2_ffn_w1_w': _L2_ffn_in['w1_w'], 'L2_ffn_w1_s': _L2_ffn_in['w1_s'], 'L2_ffn_w2_w': _L2_ffn_in['w2_w'], 'L2_ffn_w2_s': _L2_ffn_in['w2_s'], 'L2_ffn_h1_w': _L2_ffn_in['h1_w'], 'L2_ffn_h1_s': _L2_ffn_in['h1_s'], 'L2_ffn_h2_w': _L2_ffn_in['h2_w'], 'L2_ffn_h2_s': _L2_ffn_in['h2_s'], 'L2_ffn_w3_w': _L2_ffn_in['w3_w'], 'L2_ffn_w3_s': _L2_ffn_in['w3_s'], 'L3_attn_xw': _L3_attn_in['xw'], 'L3_attn_rW': _L3_attn_in['rW'], 'L3_attn_kW': _L3_attn_in['kW'], 'L3_attn_vW': _L3_attn_in['vW'], 'L3_attn_gW': _L3_attn_in['gW'], 'L3_attn_r_la': _L3_attn_in['r_la'], 'L3_attn_r_lb': _L3_attn_in['r_lb'], 'L3_attn_r_ll': _L3_attn_in['r_ll'], 'L3_attn_k_la': _L3_attn_in['k_la'], 'L3_attn_k_lb': _L3_attn_in['k_lb'], 'L3_attn_k_ll': _L3_attn_in['k_ll'], 'L3_attn_v_la': _L3_attn_in['v_la'], 'L3_attn_v_lb': _L3_attn_in['v_lb'], 'L3_attn_v_ll': _L3_attn_in['v_ll'], 'L3_attn_g_la': _L3_attn_in['g_la'], 'L3_attn_g_lb': _L3_attn_in['g_lb'], 'L3_attn_g_ll': _L3_attn_in['g_ll'], 'L3_attn_d_la': _L3_attn_in['d_la'], 'L3_attn_d_lb': _L3_attn_in['d_lb'], 'L3_attn_d_ll': _L3_attn_in['d_ll'], 'L3_attn_ln_w': _L3_attn_in['ln_w'], 'L3_attn_ln_b': _L3_attn_in['ln_b'], 'L3_attn_oW': _L3_attn_in['oW'], 'L3_attn_init_state': _L3_attn_in['init_state'], 'L3_attn_u': _L3_attn_in['u'], 'L3_ffn_W1': _L3_ffn_in['W1'], 'L3_ffn_b1': _L3_ffn_in['b1'], 'L3_ffn_W2': _L3_ffn_in['W2'], 'L3_ffn_b2': _L3_ffn_in['b2']}
    _x0 = _d['L0_attn_x']
    _d['L0_attn_x'] = jax.random.normal(jax.random.fold_in(jax.random.key(seed), 1), (8, 512, 128), dtype=_x0.dtype)
    del _x0
    return _d

def reference(L0_attn_x, L0_attn_Wqkv, L0_attn_Wproj, L0_attn_bproj, L0_attn_q_scale, L0_attn_k_scale, L0_ffn_gate_w, L0_ffn_gate_b, L0_ffn_expert_w, L0_ffn_expert_b, L1_attn_Wq, L1_attn_bq, L1_attn_Wk, L1_attn_bk, L1_attn_Wv, L1_attn_bv, L1_attn_decay, L1_attn_Wo, L1_attn_bo, L1_ffn_gate_w, L1_ffn_w1, L1_ffn_w2, L2_attn_Wq, L2_attn_Wk, L2_attn_Wv, L2_ffn_w1_w, L2_ffn_w1_s, L2_ffn_w2_w, L2_ffn_w2_s, L2_ffn_h1_w, L2_ffn_h1_s, L2_ffn_h2_w, L2_ffn_h2_s, L2_ffn_w3_w, L2_ffn_w3_s, L3_attn_xw, L3_attn_rW, L3_attn_kW, L3_attn_vW, L3_attn_gW, L3_attn_r_la, L3_attn_r_lb, L3_attn_r_ll, L3_attn_k_la, L3_attn_k_lb, L3_attn_k_ll, L3_attn_v_la, L3_attn_v_lb, L3_attn_v_ll, L3_attn_g_la, L3_attn_g_lb, L3_attn_g_ll, L3_attn_d_la, L3_attn_d_lb, L3_attn_d_ll, L3_attn_ln_w, L3_attn_ln_b, L3_attn_oW, L3_attn_init_state, L3_attn_u, L3_ffn_W1, L3_ffn_b1, L3_ffn_W2, L3_ffn_b2):

    def _L0_attn_ref(x, Wqkv, Wproj, bproj, q_scale, k_scale):
        import jax, jax.numpy as jnp
        import numpy as np
        EPS = 1e-08

        def rms_norm(x, scale):
            d = x.shape[-1]
            norm = jnp.linalg.norm(x, ord=2, axis=-1, keepdims=True)
            rms = norm * d ** (-0.5)
            return scale * (x / (rms + EPS))
        B, N, C = x.shape
        H = 16
        hd = C // H
        scale = hd ** (-0.5)
        qkv = (x @ Wqkv).reshape(B, N, 3, H, hd)
        qkv = jnp.transpose(qkv, (2, 0, 3, 1, 4))
        q, k, v = (qkv[0], qkv[1], qkv[2])
        q = rms_norm(q, q_scale)
        k = rms_norm(k, k_scale)
        attn = jnp.einsum('bhnc,bhmc->bhnm', q, k) * scale
        attn = jax.nn.softmax(attn, axis=-1)
        out = jnp.einsum('bhnm,bhmc->bhnc', attn, v)
        out = jnp.transpose(out, (0, 2, 1, 3)).reshape(B, N, C)
        return out @ Wproj + bproj

    def _L0_ffn_ref(inputs, gate_w, gate_b, expert_w, expert_b):
        import jax, jax.numpy as jnp
        import numpy as np
        NUM_TRUE = 8
        NUM_NULL = 2
        NUM_EXPERTS = NUM_TRUE + NUM_NULL
        TOP_K = 2
        D = inputs.shape[-1]
        x = inputs.reshape(-1, D)
        gate_logits = x @ gate_w.T + gate_b
        gate_probs = jax.nn.softmax(gate_logits, axis=-1)
        weights, selected = jax.lax.top_k(gate_probs, TOP_K)
        true_mask = selected < NUM_TRUE
        true_weights = weights * true_mask
        denom = true_weights.sum(axis=-1, keepdims=True)
        denom = jnp.where(denom > 0, denom, jnp.ones_like(denom))
        norm_w = (true_weights / denom).astype(x.dtype)
        one_hot = jax.nn.one_hot(selected, NUM_EXPERTS, dtype=norm_w.dtype)
        combine_w = jnp.einsum('tk,tke->te', norm_w, one_hot)[:, :NUM_TRUE]
        expert_out = jnp.einsum('td,edh->teh', x, expert_w) + expert_b[None, :, :]
        out = jnp.einsum('te,teh->th', combine_w, expert_out)
        return out.reshape(inputs.shape[:-1] + (out.shape[-1],))

    def _L1_attn_ref(x, Wq, bq, Wk, bk, Wv, bv, decay, Wo, bo):
        import jax, jax.numpy as jnp
        import numpy as np
        B, T, D, DS = (8, 512, 128, 64)
        q = jnp.einsum('btd,sd->bts', x, Wq) + bq
        k = jnp.einsum('btd,sd->bts', x, Wk) + bk
        v = jnp.einsum('btd,sd->bts', x, Wv) + bv
        d = jax.nn.sigmoid(decay)

        def step(S, qkv_t):
            q_t, k_t, v_t = qkv_t
            S = d[None, :, None] * S + v_t[:, :, None] * k_t[:, None, :]
            o = jnp.einsum('bij,bj->bi', S, q_t)
            return (S, o)
        S0 = jnp.zeros((x.shape[0], d.shape[0], d.shape[0]), dtype=x.dtype)
        qkv = (jnp.swapaxes(q, 0, 1), jnp.swapaxes(k, 0, 1), jnp.swapaxes(v, 0, 1))
        _, outs = jax.lax.scan(step, S0, qkv)
        scan_out = jnp.swapaxes(outs, 0, 1)
        return x + jnp.einsum('bts,ds->btd', scan_out, Wo) + bo

    def _L1_ffn_ref(x, gate_w, w1, w2):
        import math
        import jax, jax.numpy as jnp
        import numpy as np
        D_MODEL = 128
        NUM_EXPERTS = 8
        D_FF_EXPERT = max(64, int(D_MODEL * 4 * 0.25))
        THRESHOLD = 0.9
        CAP_FACTOR = 1.0
        INIT_STD = 0.02

        def _xmoe_route(probs):
            N, E = probs.shape
            order = jnp.argsort(-probs, axis=-1)
            p_sorted = jnp.take_along_axis(probs, order, axis=-1)
            csum = jnp.cumsum(p_sorted, axis=-1)
            reached = (csum >= THRESHOLD).at[:, -1].set(True)
            k_idx = jnp.argmax(reached, axis=-1)
            select_prefix = jnp.arange(E)[None, :] <= k_idx[:, None]
            rows = jnp.arange(N)[:, None]
            assign_mask = jnp.zeros((N, E), dtype=bool).at[rows, order].set(select_prefix)
            rank = jnp.arange(1, E + 1, dtype=probs.dtype)[None, :]
            R_sorted = jnp.where(select_prefix, p_sorted - rank, jnp.full_like(p_sorted, -1000000000.0))
            R = jnp.zeros((N, E), dtype=probs.dtype).at[rows, order].set(R_sorted)
            capacity = int(math.ceil(N / E) * CAP_FACTOR)
            C = min(capacity, N)
            tok_order = jnp.argsort(-R, axis=0)
            topC = tok_order[:C, :]
            keep = jnp.zeros((N, E), dtype=bool).at[topC, jnp.arange(E)[None, :]].set(True)
            final_mask = assign_mask & keep
            return jnp.where(final_mask, probs, jnp.zeros_like(probs))
        B, T, D = x.shape
        N = B * T
        xf = x.reshape(N, D)
        probs = jax.nn.softmax(xf @ gate_w.T, axis=-1)
        scores_sel = _xmoe_route(probs)
        h = jax.nn.gelu(jnp.einsum('nd,efd->enf', xf, w1), approximate=False)
        y_e = jnp.einsum('enf,edf->end', h, w2)
        y = jnp.einsum('ne,end->nd', scores_sel, y_e)
        return y.reshape(B, T, D)

    def _L2_attn_ref(x, Wq, Wk, Wv):
        import jax, jax.numpy as jnp
        import numpy as np
        B, N = (2, 256)
        H, R = (8, 64)
        IN_DIM, OUT_DIM = (64, 64)
        D = IN_DIM + OUT_DIM
        INIT = 1.0
        b, n, d = x.shape
        Q = (x @ Wq.T).reshape(b, n, H, R)
        K = (x @ Wk.T).reshape(b, n, H, R)
        V = (x @ Wv.T).reshape(b, n, H, d)
        attn = jnp.einsum('bnhr,bmhr->bhnm', Q, K)
        attn = jax.nn.softmax(attn, axis=-1)
        out = jnp.einsum('bhnm,bmhd->bnd', attn, V)
        return out

    def _L2_ffn_ref(x, w1_w, w1_s, w2_w, w2_s, h1_w, h1_s, h2_w, h2_s, w3_w, w3_s):
        import jax, jax.numpy as jnp
        import numpy as np
        D_IN, D_HID = (128, 512)

        def _ternary(key, shape):
            return jax.random.randint(key, shape, -1, 2).astype(jnp.float32)

        def _tlin(x, w, s):
            return jnp.einsum('bsi,oi->bso', x, w) * s
        h = jax.nn.silu(_tlin(x, w1_w, w1_s)) * _tlin(x, w2_w, w2_s)
        h = jax.nn.gelu(_tlin(h, h1_w, h1_s), approximate=False)
        h = jax.nn.gelu(_tlin(h, h2_w, h2_s), approximate=False)
        return _tlin(h, w3_w, w3_s)

    def _L3_attn_ref(x, xw, rW, kW, vW, gW, r_la, r_lb, r_ll, k_la, k_lb, k_ll, v_la, v_lb, v_ll, g_la, g_lb, g_ll, d_la, d_lb, d_ll, ln_w, ln_b, oW, init_state, u):
        import jax, jax.numpy as jnp
        import numpy as np
        B, T, D, H, LORA = (4, 128, 128, 16, 64)
        HD = D // H
        BLOCK_ID, N_BLOCKS = (6, 12)

        def _ln(x, w, b, eps=1e-05):
            m = x.mean(-1, keepdims=True)
            v = ((x - m) ** 2).mean(-1, keepdims=True)
            return (x - m) * jax.lax.rsqrt(v + eps) * w + b

        def _lora(z, a, b, l):
            return l + jnp.tanh(z @ a.T) @ b.T

        def _reference_tuple_inner(x, xw, rW, kW, vW, gW, r_la, r_lb, r_ll, k_la, k_lb, k_ll, v_la, v_lb, v_ll, g_la, g_lb, g_ll, d_la, d_lb, d_ll, ln_w, ln_b, oW, init_state, u):
            b, t, d = x.shape
            h = init_state.shape[0]
            hd = d // h
            xx = jnp.concatenate([jnp.zeros_like(x[:, :1]), x[:, :-1]], axis=1)
            dx = xx - x
            lerpx = x + dx * xw
            r = (x + dx * _lora(lerpx, r_la, r_lb, r_ll)) @ rW.T
            k = (x + dx * _lora(lerpx, k_la, k_lb, k_ll)) @ kW.T
            v = (x + dx * _lora(lerpx, v_la, v_lb, v_ll)) @ vW.T
            g = (x + dx * _lora(lerpx, g_la, g_lb, g_ll)) @ gW.T
            w = jnp.exp(-jnp.exp(_lora(x + dx * _lora(lerpx, d_la, d_lb, d_ll), d_la, d_lb, d_ll)))
            split = lambda z: z.reshape(b, t, h, hd).transpose(1, 0, 2, 3)
            rs, ws, ks, vs = (split(r), split(w), split(k), split(v))
            uh = u.reshape(h, hd)
            st0 = jnp.broadcast_to(init_state, (b, h, hd, hd))

            def step(st, inp):
                rt, wt, kt, vt = inp
                kv = jnp.einsum('bhi,bhj->bhij', kt, vt)
                y = jnp.einsum('bhi,bhij->bhj', rt, st + uh[None, :, :, None] * kv)
                return (wt[..., None] * st + kv, y)
            st1, ys = jax.lax.scan(step, st0, (rs, ws, ks, vs))
            o = jax.nn.silu(g.reshape(b, t, h, hd)) * _ln(ys.transpose(1, 0, 2, 3), ln_w, ln_b)
            return (o.reshape(b, t, d) @ oW.T, st1)
        return _reference_tuple_inner(x, xw, rW, kW, vW, gW, r_la, r_lb, r_ll, k_la, k_lb, k_ll, v_la, v_lb, v_ll, g_la, g_lb, g_ll, d_la, d_lb, d_ll, ln_w, ln_b, oW, init_state, u)[0]

    def _L3_ffn_ref(x, W1, b1, W2, b2):
        import jax, jax.numpy as jnp
        import numpy as np
        EMB = 128
        FF = 4 * EMB

        def _ternary(w):
            scale = jnp.maximum(jnp.mean(jnp.abs(w)), 1e-08)
            w_t = jnp.clip(jnp.round(w / scale), -1.0, 1.0)
            return w + jax.lax.stop_gradient(w_t - w)
        h = jnp.einsum('bsd,fd->bsf', x, _ternary(W1)) + b1
        h = jax.nn.gelu(h, approximate=False)
        out = jnp.einsum('bsf,df->bsd', h, _ternary(W2)) + b2
        return out
    x = L0_attn_x
    xn = _layernorm(x, axis=-1)
    x = x + _L0_attn_ref(xn, L0_attn_Wqkv, L0_attn_Wproj, L0_attn_bproj, L0_attn_q_scale, L0_attn_k_scale) + _L0_ffn_ref(xn, L0_ffn_gate_w, L0_ffn_gate_b, L0_ffn_expert_w, L0_ffn_expert_b)
    xn = _layernorm(x, axis=-1)
    x = x + _L1_attn_ref(xn, L1_attn_Wq, L1_attn_bq, L1_attn_Wk, L1_attn_bk, L1_attn_Wv, L1_attn_bv, L1_attn_decay, L1_attn_Wo, L1_attn_bo) + _L1_ffn_ref(xn, L1_ffn_gate_w, L1_ffn_w1, L1_ffn_w2)
    xn = _layernorm(x, axis=-1)
    x = x + _L2_attn_ref(xn, L2_attn_Wq, L2_attn_Wk, L2_attn_Wv) + _L2_ffn_ref(xn, L2_ffn_w1_w, L2_ffn_w1_s, L2_ffn_w2_w, L2_ffn_w2_s, L2_ffn_h1_w, L2_ffn_h1_s, L2_ffn_h2_w, L2_ffn_h2_s, L2_ffn_w3_w, L2_ffn_w3_s)
    xn = _layernorm(x, axis=-1)
    x = x + _L3_attn_ref(xn, L3_attn_xw, L3_attn_rW, L3_attn_kW, L3_attn_vW, L3_attn_gW, L3_attn_r_la, L3_attn_r_lb, L3_attn_r_ll, L3_attn_k_la, L3_attn_k_lb, L3_attn_k_ll, L3_attn_v_la, L3_attn_v_lb, L3_attn_v_ll, L3_attn_g_la, L3_attn_g_lb, L3_attn_g_ll, L3_attn_d_la, L3_attn_d_lb, L3_attn_d_ll, L3_attn_ln_w, L3_attn_ln_b, L3_attn_oW, L3_attn_init_state, L3_attn_u) + _L3_ffn_ref(xn, L3_ffn_W1, L3_ffn_b1, L3_ffn_W2, L3_ffn_b2)
    return x

_drawn_inputs = setup_inputs


def setup_inputs(seed=0):
    import zlib

    import numpy as np

    out = dict(_drawn_inputs(seed))
    spreads = {'L0_attn_bproj': (0.0, 0.1),
     'L0_attn_q_scale': (1.0, 0.2),
     'L0_attn_k_scale': (1.0, 0.2),
     'L0_ffn_gate_b': (0.0, 0.1),
     'L0_ffn_expert_b': (0.0, 0.1),
     'L1_attn_bq': (0.0, 0.1),
     'L1_attn_bk': (0.0, 0.1),
     'L1_attn_bv': (0.0, 0.1),
     'L1_attn_decay': (0.949999988079071, 0.2),
     'L1_attn_bo': (0.0, 0.1),
     'L3_attn_ln_w': (0.6857119798660278, 0.2),
     'L3_attn_ln_b': (0.0, 0.1)}
    factors = {}
    for name, (base, spread) in spreads.items():
        noise = np.random.default_rng([zlib.crc32(name.encode()), seed]).standard_normal(out[name].shape)
        drawn = base * np.exp(spread * noise) if base else spread * noise
        out[name] = jnp.asarray(drawn.astype(out[name].dtype))
    for name, factor in factors.items():
        out[name] = (out[name] * factor).astype(out[name].dtype)
    return out
```

```python
from contextlib import ExitStack

import numpy as np
import concourse.bass as bass
from concourse import mybir

F32 = mybir.dt.float32
BF16 = mybir.dt.bfloat16
ALU = mybir.AluOpType
ACT = mybir.ActivationFunctionType
AX_X = mybir.AxisListType.X

B, T, D = 8, 512, 128
NTOK = B * T
P = 128
NBLK = T // P
NT = NTOK // P
EPS = 1e-5

H0, HD0 = 16, 8
E0, E0_TRUE = 10, 8
E1, F1 = 8, 128
DS = 64
C1 = 64
NC1 = T // C1
CAP = NTOK // E1
H2, R2 = 8, 64
FF = 512
FT = FF // P
H3, HD3 = 16, 8


def pad_rows(a):
    out = np.zeros((P,) + a.shape[1:], np.float32)
    out[: a.shape[0]] = a
    return out


def col(a):
    return pad_rows(np.asarray(a, np.float32).reshape(-1, 1))


def row(a):
    return np.broadcast_to(np.asarray(a, np.float32).reshape(1, -1), (P, np.size(a)))


def tiles_of_rows(a):
    n = a.shape[0] // P
    return a.reshape(n, P, a.shape[1]).transpose(1, 0, 2).reshape(P, -1)


def constants():
    i = np.arange(P)
    same8 = (i[:, None] // 8 == i[None, :] // 8).astype(np.float32)
    c = {"ident": np.eye(P, dtype=np.float32), "mean_all": np.full((P, P), 1 / D, np.float32),
         "mean_head": same8 / 8, "sum_head": same8}
    num, den = np.zeros((P, 4, P), np.float32), np.zeros((P, 4, P), np.float32)
    for g in range(4):
        for j in range(4):
            for k in range(8):
                num[32 * j + k, g, (4 * g + j) * 8 + k] = 1
                den[32 * j + 8, g, (4 * g + j) * 8 + k] = 1
    c["place_num"], c["place_den"] = num.reshape(P, -1), den.reshape(P, -1)
    e, g = i // 16, i % 16
    c["sum_expert"] = (e[:, None] == e[None, :]).astype(np.float32)
    c["before_group"] = ((e[:, None] == e[None, :]) & (g[:, None] < g[None, :])).astype(np.float32)
    t = np.arange(C1)
    c["chunk_o_pow"] = row(t - C1 // 2)
    c["chunk_v_pow"] = (C1 // 2 - i % C1).astype(np.float32).reshape(P, 1)
    same_chunk = i[:, None] // C1 == i[None, :] // C1
    c["causal"] = (same_chunk & (i[None, :] >= i[:, None])).astype(np.float32)
    c["chunk_of"] = (i[:, None] // C1 == np.arange(P // C1)[None, :]).astype(np.float32)
    pick = np.zeros((P, 8, P), np.float32)
    for j in range(8):
        pick[i, j, (i // 8) * 8 + j] = 1
    c["pick_j"] = pick.reshape(P, -1)
    return c


def packed(v):
    f = {k: np.asarray(a) for k, a in v.items()}
    k = constants()
    wqkv = f["L0_attn_Wqkv"]
    common = {"mean_all": k["mean_all"], "ident": k["ident"], "mean_head": k["mean_head"]}
    first = {
        "gate0": f["L0_ffn_gate_w"].T, "gate0_b": row(f["L0_ffn_gate_b"]),
        "wq0": wqkv[:, 0:D], "wk0": wqkv[:, D:2 * D], "wv0": wqkv[:, 2 * D:],
        "wproj0": f["L0_attn_Wproj"], "bproj0": col(f["L0_attn_bproj"]),
        "qs_col": col(np.tile(f["L0_attn_q_scale"], H0)), "ks_col": col(np.tile(f["L0_attn_k_scale"], H0)),
        "qs_row": row(f["L0_attn_q_scale"]), "ks_row": row(f["L0_attn_k_scale"]),
        "place_num": k["place_num"], "place_den": k["place_den"],
        "expert0": f["L0_ffn_expert_w"].transpose(1, 0, 2).reshape(P, -1),
        "expert0_b": pad_rows(f["L0_ffn_expert_b"]),
    }
    second = {
        "ways": row(np.arange(1, 8)), "gate1": f["L1_ffn_gate_w"].T,
        "sum_expert": k["sum_expert"], "before_group": k["before_group"],
        "wq1": f["L1_attn_Wq"].T, "wk1": f["L1_attn_Wk"].T,
        "wkv1": np.concatenate([f["L1_attn_Wk"].T, f["L1_attn_Wv"].T], 1),
        "bq1": col(f["L1_attn_bq"]), "bk1": col(f["L1_attn_bk"]),
        "bkv1": row(np.concatenate([f["L1_attn_bk"], f["L1_attn_bv"]])),
        "wo1": pad_rows(f["L1_attn_Wo"].T), "bo1": col(f["L1_attn_bo"]),
        "decay_col": col(f["L1_attn_decay"]), "decay_row": row(f["L1_attn_decay"]),
        "chunk_o_pow": k["chunk_o_pow"], "chunk_v_pow": k["chunk_v_pow"], "causal": k["causal"], "chunk_of": k["chunk_of"],
        "up1": f["L1_ffn_w1"].transpose(2, 0, 1).reshape(P, -1),
        "down1": f["L1_ffn_w2"].transpose(2, 0, 1).reshape(P, -1),
    }
    third = {
        "wq2": f["L2_attn_Wq"].T, "wk2": f["L2_attn_Wk"].T, "wv2": f["L2_attn_Wv"].T,
        "w1_2": f["L2_ffn_w1_w"].T, "w2_2": f["L2_ffn_w2_w"].T,
        "h1_2": tiles_of_rows(f["L2_ffn_h1_w"].T),
    }
    third_whole = {
        "h2_2": tiles_of_rows(f["L2_ffn_h2_w"].T),
        "w3_2": tiles_of_rows(f["L2_ffn_w3_w"].T),
        "s1_2": f["L2_ffn_w1_s"].reshape(FT, P).T, "s2_2": f["L2_ffn_w2_s"].reshape(FT, P).T,
        "sh1_2": f["L2_ffn_h1_s"].reshape(FT, P).T, "sh2_2": f["L2_ffn_h2_s"].reshape(FT, P).T,
        "s3_2": col(f["L2_ffn_w3_s"]),
    }
    z = np.zeros((P, P), np.float32)
    la = {n: f[f"L3_attn_{n}_la"].T for n in "rkvgd"}

    def lb(n, low):
        a = z.copy()
        a[0 if low else 64:64 if low else P] = f[f"L3_attn_{n}_lb"].T
        return a

    vw = f["L3_attn_vW"].T
    spread = (np.arange(P) // 8)[None, :] * 8 + np.arange(8)[:, None]
    fourth = {
        "sum_head": k["sum_head"], "pick_j": k["pick_j"],
        "xw": col(f["L3_attn_xw"]),
        "la_rk": np.concatenate([la["r"], la["k"]], 1), "la_vg": np.concatenate([la["v"], la["g"]], 1),
        "la_d": np.concatenate([la["d"], z[:, :64]], 1),
        "lb_r": lb("r", True), "lb_k": lb("k", False), "lb_v": lb("v", True), "lb_g": lb("g", False),
        "lb_d": lb("d", True),
        **{f"ll_{n}": col(f[f"L3_attn_{n}_ll"]) for n in "rkvgd"},
        "rW": f["L3_attn_rW"].T, "kW": f["L3_attn_kW"].T, "gW": f["L3_attn_gW"].T,
        "vW": vw,
        "vW_j": np.concatenate([vw[:, s] for s in spread], 1),
        "u": col(f["L3_attn_u"]),
        "state": f["L3_attn_init_state"].reshape(P, HD3),
        "ln_w": col(np.tile(f["L3_attn_ln_w"], H3)), "ln_b": col(np.tile(f["L3_attn_ln_b"], H3)),
        "oW": f["L3_attn_oW"].T,
        "W1_3": f["L3_ffn_W1"].T, "W2_3": tiles_of_rows(f["L3_ffn_W2"].T),
        "b1_3": f["L3_ffn_b1"].reshape(FT, P).T, "b2_3": col(f["L3_ffn_b2"]),
    }
    return [common, first, second, third, third_whole, fourth]


def single(a):
    return a.bitcast(mybir.dt.float32r)


def at(b, n=T):
    return bass.ts(b, n)


class Weights:

    def __init__(self, tensor, widths):
        self.tensor, self.part, c = tensor, {}, 0
        for name, n in widths.items():
            self.part[name] = (c, n)
            c += n
        self.width = c

    def __getitem__(self, name):
        c, n = self.part[name]
        return self.tensor[:, c:c + n]


def layer_norm(nc, ctx, sh, xc, ps, x_loaded=None):
    mean_done, centred, squared, var_done, rstd_done, normed = (
        ctx.enter_context(nc.semaphore(n))
        for n in ("mean_done", "centred", "squared", "var_done", "rstd_done", "normed"))
    x, xn, w = sh["x"], sh["xn"], sh["common"]

    def ahead(eng, n, first, second, between=None):
        for b in range(n):
            first(b)
        if between:
            between(eng)
        with eng.Fori(0, B - n) as b:
            first(b + n)
            second(b)
        for b in range(B - n, B):
            second(b)

    def tensor(pe):
        def mean(b):
            nc.tensor.matmul(ps[:, b, :], w["mean_all"], x[:, at(b)], start=True, stop=True).then_inc(mean_done, 1)

        def variance(b):
            pe.wait_ge(squared, b + 1)
            nc.tensor.matmul(ps[:, b, :], w["mean_all"], xn[:, at(b)], start=True, stop=True).then_inc(var_done, 1)

        def between(pe):
            if x_loaded is not None:
                pe.wait_ge(x_loaded[1], 16)

        pe.wait_ge(sh["common_loaded"], 16)
        if x_loaded is not None:
            pe.wait_ge(x_loaded[0], 16)
        ahead(pe, 3, mean, variance, between)

    def vector(dve):
        def centre(b):
            dve.wait_ge(mean_done, b + 1)
            nc.vector.tensor_tensor(xc[:, at(b)], x[:, at(b)], ps[:, b, :], ALU.subtract).then_inc(centred, 1)

        def scale(b):
            dve.wait_ge(rstd_done, b + 1)
            nc.vector.tensor_tensor(xn[:, at(b)], xc[:, at(b)], xn[:, at(b)], ALU.mult).then_inc(normed, 1)

        ahead(dve, 4, centre, scale)

    def scalar(act):
        def square(b):
            act.wait_ge(centred, b + 1)
            nc.scalar.activation(xn[:, at(b)], xc[:, at(b)], ACT.Square).then_inc(squared, 1)

        def rstd(b):
            act.wait_ge(var_done, b + 1)
            nc.scalar.activation(xn[:, at(b)], ps[:, b, :], ACT.Ln, bias=sh["eps"][:, 0:1])
            act.drain()
            nc.scalar.activation(xn[:, at(b)], xn[:, at(b)], ACT.Exp, scale=-0.5).then_inc(rstd_done, 1)

        act.wait_ge(sh["eps_set"], 2)
        ahead(act, 2, square, rstd)

    return tensor, vector, scalar, normed


def gate_logits(nc, pe, xn, gate, ps, n, normed, done):
    for t in range(NT):
        if t % NBLK == 0:
            pe.wait_ge(normed, t // NBLK + 1)
        last = nc.tensor.matmul(ps[:, 0, t * n:(t + 1) * n], xn[:, t * P:(t + 1) * P], gate,
                                start=True, stop=True)
    last.then_inc(done, 1)


def over(a, n):
    return a.unsqueeze(2).broadcast_to([a.shape[0], a.shape[1], n])


def probabilities(nc, dve, lg, stat, exped_in, exped, n):
    nc.vector.reduce_max(stat[:, 0:NT], lg[:, :, :], AX_X)
    dve.drain()
    nc.vector.tensor_tensor(lg[:, :, :], lg[:, :, :], over(stat[:, 0:NT], n), ALU.subtract).then_inc(exped_in, 1)
    dve.wait_ge(exped, 1)
    nc.vector.reduce_sum(stat[:, 0:NT], lg[:, :, :], AX_X)
    dve.drain()
    nc.vector.reciprocal(stat[:, NT:2 * NT], stat[:, 0:NT])
    dve.drain()
    nc.vector.tensor_tensor(lg[:, :, :], lg[:, :, :], over(stat[:, NT:2 * NT], n), ALU.mult)
    dve.drain()


def precedence(nc, dve, p, first, n):
    for e in range(n):
        for others, before in ((slice(0, e), ALU.is_ge), (slice(e, n), ALU.is_gt)):
            count = others.stop - others.start
            if count:
                nc.vector.tensor_tensor(first[:, :, e, others], p[:, :, others], over(p[:, :, e], count), before)
    dve.drain()


def layer0_norm(nc, sh):
    x, xn, w = sh["x"], sh["xn"], sh["w"][0]
    with ExitStack() as ctx:
        xc = ctx.enter_context(nc.sbuf_tensor("n0_xc", [P, NTOK], F32))
        ps = ctx.enter_context(nc.psum_tensor("n0_ps", [P, 8, 512], F32))
        logits_done = ctx.enter_context(nc.semaphore("logits_done"))
        ln_pe, ln_dve, ln_act, normed = layer_norm(nc, ctx, sh, xc, ps, sh["x_loaded"])
        block = ctx.enter_context(nc.Block())

        @block.sync
        def _(sp):
            sp.dma_start(sh["common"].tensor[:, :], sh["common_dram"]).then_inc(sh["common_loaded"], 16)
            for half in range(2):
                cols = slice(half * NTOK // 2, (half + 1) * NTOK // 2)
                sp.dma_start(x[:, cols], sh["x_dram"][:, cols]).then_inc(sh["x_loaded"][half], 16)
            sp.dma_start(w.tensor[:, :], sh["w_dram"][0]).then_inc(sh["w_loaded"][0], 16)

        @block.tensor
        def _(pe):
            ln_pe(pe)
            pe.wait_ge(sh["w_loaded"][0], 16)
            gate_logits(nc, pe, xn, w["gate0"], ps, E0, normed, logits_done)

        @block.scalar
        def _(act):
            nc.scalar.preload_act_table_set("natural_log_exp_and_others")
            ln_act(act)

        @block.vector
        def _(dve):
            nc.vector.memset(sh["eps"][:, 0:1], EPS).then_inc(sh["eps_set"], 1)
            nc.vector.memset(sh["eps"][:, 1:2], 1.0).then_inc(sh["eps_set"], 1)
            ln_dve(dve)
            dve.wait_ge(logits_done, 1)
            nc.vector.tensor_tensor(sh["logits0"][:, :, :], ps[:, 0, 0:NT * E0].rearrange("p (t e) -> p t e", e=E0),
                                    w["gate0_b"].unsqueeze(1).broadcast_to([P, NT, E0]), ALU.add)


Q_RUNS = [(0, 3, True), (0, 2, True), (0, 1, True)]
K_RUNS = [(0, 3, False), (1, 2, False), (2, 1, False)]
SLOTS = 6
SETS = H0
BOUND0 = float(HD0) ** 0.5


def layer0_mix(nc, sh):
    x, xn, w = sh["x"], sh["xn"], sh["w"][0]
    with ExitStack() as ctx:
        sb = lambda name, shape, dt=F32: ctx.enter_context(nc.sbuf_tensor(name, shape, dt))
        sem = lambda name: ctx.enter_context(nc.semaphore(name))
        q_stack = [sb(f"q_stack{i}", [P, H0, T], BF16) for i in range(2)]
        k_stack = [sb(f"k_stack{i}", [P, H0, T], BF16) for i in range(2)]
        v = [sb(f"v{i}", [P, NBLK, H0, 32]) for i in range(2)]
        probs = [sb(f"probs{i}", [P, 4, T]) for i in range(2)]
        xst = sb("xst", [P, T])
        qk = sb("qk", [P, 2, T])
        sq = sb("sq", [P, 2, T])
        inv = sb("inv", [P, T])
        parts = sb("parts", [P, 2, 3, T], BF16)
        o_sb = sb("o_sb", [P, 4, T])
        on = sb("on", [P, T])
        rden = sb("rden", [P, T])
        cwb = sb("cwb", [P, E0_TRUE, T])
        cwT = sb("cwT", [E0_TRUE, T])
        lg, rank = sh["logits0"], sb("rank0", [P, NT, E0])
        first = cwb[:, :, :].rearrange("p e t -> p (e t)")[:, 0:NT * E0 * E0].rearrange("p (t e f) -> p t e f", t=NT, e=E0)
        stat, cw, cw_rows = sb("stat0", [P, 3 * NT]), sb("cw0", [P, NT, E0_TRUE]), sb("cw_rows0", [P, 2, P])
        xe = sb("xe", [P, 2, T])
        bound = sb("bound", [P, 10])
        ps_s = ctx.enter_context(nc.psum_tensor("ps_s", [P, 4, 512], F32))
        ps_o = ctx.enter_context(nc.psum_tensor("ps_o", [P, 512], F32))
        ps_m = ctx.enter_context(nc.psum_tensor("ps_m", [P, 512], F32))
        ps_d = ctx.enter_context(nc.psum_tensor("ps_d", [P, 512], F32))
        ps_y = ctx.enter_context(nc.psum_tensor("ps_y", [P, 512], F32))

        filled = sem("filled")
        filled1 = sem("filled1")
        xst_ready = sem("xst_ready")
        misc_done = sem("misc_done")
        misc_read = sem("misc_read")
        ms_read = sem("ms_read")
        squared = sem("squared")
        inv_read = sem("inv_read")
        parts_ready = sem("parts_ready")
        scratch_written = sem("scratch_written")
        stack_ready = sem("stack_ready")
        scored = sem("scored")
        exped = sem("exped")
        pv_done = sem("pv_done")
        o_copied = sem("o_copied")
        nd_done = sem("nd_done")
        on_ready = sem("on_ready")
        xe_ready = sem("xe_ready")
        xe_used = sem("xe_used")
        y_done = sem("y_done")
        x_added = sem("x_added")
        cw_loaded = sem("cw_loaded")
        biased = sem("biased")
        bound_ready = sem("bound_ready")
        exp_in, exp_out, combined, turned, cw_ready, cw_stored = (
            sem(n) for n in ("exp_in", "exp_out", "combined", "turned", "cw_rows_ready", "cw_stored"))
        block = ctx.enter_context(nc.Block())

        @block.sync
        def _(sp):
            def ahead(value):
                return value if isinstance(value, int) else sp.snap(value)

            def load_cw(b):
                start, weighed, biases = ahead(b * T), ahead(b * E0_TRUE), ahead(b * 1)
                sp.wait_ge(xe_ready, weighed)
                sp.wait_ge(biased, biases)
                here = sh["cw_dram"][:, bass.ds(start, T)]
                sp.dma_start(cwb[:, :, :], here.unsqueeze(0).broadcast_to([P, E0_TRUE, T])).then_inc(cw_loaded, 16)
                sp.dma_start(cwT[:, :], here).then_inc(cw_loaded, 16)

            def stack(b, buf):
                before, split_q, split_k = ahead(b * 96), ahead(b * 2 + 1), ahead(b * 2 + 2)
                written = ahead(b * 96 + 96)
                sp.wait_ge(stack_ready, before)
                for n, ready in ((0, split_q), (1, split_k)):
                    sp.wait_ge(parts_ready, ready)
                    for part in range(3):
                        sp.dma_start(sh["parts_dram"][n, part].rearrange("c h n -> h c n"),
                                     parts[:, n, part, :]).then_inc(scratch_written, 16)
                sp.wait_ge(scratch_written, written)
                for n, runs, to in ((0, Q_RUNS, q_stack[buf]), (1, K_RUNS, k_stack[buf])):
                    row0 = 0
                    for part, count, ascending in runs:
                        src = sh["parts_dram"][n, 0:count].rearrange("s c h n -> (s c) h n") if ascending else \
                            sh["parts_dram"][n, part:part + 1].broadcast_to([count, HD0, H0, T])
                        sp.dma_start(to[row0:row0 + 8 * count, :, :], src).then_inc(stack_ready, 16)
                        row0 += 8 * count

            sp.wait_ge(filled, 6)
            stack(0, 0)
            sp.wait_ge(cw_ready, 1)
            to = sh["cw_dram"].rearrange("e (k t p) -> k t e p", k=2, p=P)
            for k in range(2):
                sp.dma_start(to[k], cw_rows[:, k, :]).then_inc(cw_stored, 16)
            sp.wait_ge(cw_stored, 32)
            load_cw(0)
            sp.wait_ge(filled1, 2)
            stack(1, 1)
            with sp.Fori(1, B - 1, 2) as b:
                for k in range(2):
                    load_cw(b + k)
                    stack(b + k + 1, k)
            load_cw(B - 1)

        @block.gpsimd
        def _(pool):
            def prologue(b):
                pool.wait_ge(misc_done, b * 5)
                nc.gpsimd.tensor_copy(xst[:, :], xn[:, at(b)]).then_inc(xst_ready, 1)
                for n in range(2):
                    pool.wait_ge(misc_read, b * 3 + n + 1)
                    nc.gpsimd.tensor_tensor(sq[:, n, :], qk[:, n, :], qk[:, n, :], ALU.mult).then_inc(squared, 1)

            prologue(0)
            for t in (q_stack[1], k_stack[1]):
                pool.drain()
                nc.gpsimd.memset(t[:, :, :].bitcast(F32), 0.0).then_inc(filled1, 1)
            pool.drain()
            with pool.Fori(1, B) as b:
                prologue(b)

        @block.scalar
        def _(act):
            nc.scalar.preload_act_table_set("natural_log_exp_and_others")
            act.sem_inc(exped, 1)
            act.wait_ge(bound_ready, 1)

            def rms(b, n):
                act.wait_ge(misc_done, b * 5 + n + 4)
                act.wait_ge(inv_read, b * 2 + n)
                nc.scalar.activation(inv[:, :], ps_m[:, :], ACT.Ln, bias=bound[:, 8:9])
                act.drain()
                nc.scalar.activation(inv[:, :], inv[:, :], ACT.Exp, scale=0.5)

            def inverse_rms():
                act.drain()
                nc.scalar.activation(inv[:, :], inv[:, :], ACT.Ln, bias=bound[:, 9:10])
                act.drain()
                nc.scalar.activation(inv[:, :], inv[:, :], ACT.Exp, scale=-1.0).then_inc(ms_read, 1)

            def attend(b, nxt):
                for s in range(SETS):
                    act.wait_ge(pv_done, b * SETS + s + 15)
                    for half in range(2):
                        u = 2 * s + half
                        act.wait_ge(scored, b * 32 + u + 1)
                        nc.scalar.activation(probs[s % 2][:, 2 * half:2 * half + 2, :], ps_s[:, 2 * half:2 * half + 2, :],
                                             ACT.Exp, bias=bound[:, 7:8], scale=float(HD0) ** -0.5).then_inc(exped, 1)
                    if nxt is not None and s in (7, 9):
                        rms(nxt, (s - 7) // 2)
                    if nxt is not None and s in (8, 10):
                        inverse_rms()

            for n in range(2):
                rms(0, n)
                inverse_rms()
            act.wait_ge(exp_in, 1)
            nc.scalar.activation(lg[:, :, :], lg[:, :, :], ACT.Exp).then_inc(exp_out, 1)
            attend(0, 1)
            with act.Fori(1, B - 1, 2) as b:
                for k in range(2):
                    attend(b + k, b + k + 1)
            attend(B - 1, None)

        @block.vector
        def _(dve):
            dve.sem_inc(o_copied, 1)
            dve.sem_inc(on_ready, 1)
            for i in range(2):
                nc.vector.memset(v[i][:, :, :, 9:32], 0.0).then_inc(filled, 1)
            nc.vector.memset(v[0][:, :, :, 8:9], 1.0).then_inc(filled, 1)
            nc.vector.memset(v[1][:, :, :, 8:9], 1.0).then_inc(filled, 1)
            nc.vector.tensor_tensor(bound[:, 0:8], w["qs_row"], w["ks_row"], ALU.mult)
            dve.drain()
            nc.vector.scalar_tensor_tensor(bound[:, 0:8], bound[:, 0:8], -1.0, bound[:, 0:8], ALU.mult, ALU.max)
            dve.drain()
            nc.vector.reduce_max(bound[:, 8:9], bound[:, 0:8], AX_X)
            dve.drain()
            nc.vector.tensor_scalar(bound[:, 7:8], bound[:, 8:9], -BOUND0, None, ALU.mult)
            dve.drain()
            nc.vector.memset(bound[:, 8:9], 2.0 ** -63)
            nc.vector.memset(bound[:, 9:10], 1e-8).then_inc(bound_ready, 1)

            def read(b, n):
                dve.wait_ge(misc_done, b * 5 + n + 1)
                if n < 2:
                    dve.wait_ge(squared, b * 2 + n)
                    nc.vector.tensor_copy(qk[:, n, :], ps_m[:, :]).then_inc(misc_read, 1)

            def read_v(b, buf):
                dve.wait_ge(misc_done, b * 5 + 3)
                dve.wait_ge(pv_done, b * SETS)
                nc.vector.tensor_copy(v[buf][:, :, :, 0:8], ps_m[:, :].rearrange("p (m h c) -> p m h c", m=NBLK, c=8)
                                      ).then_inc(misc_read, 1)

            def split(b, n):
                dve.wait_ge(ms_read, b * 2 + n + 1)
                nc.vector.scalar_tensor_tensor(qk[:, n, :], qk[:, n, :], w["qs_col" if n == 0 else "ks_col"],
                                               inv[:, :], ALU.mult, ALU.mult).then_inc(inv_read, 1)
                dve.drain()
                dve.wait_ge(scratch_written, b * 96)
                nc.vector.tensor_copy(parts[:, n, 0, :], qk[:, n, :])
                dve.drain()
                nc.vector.tensor_tensor(qk[:, n, :], qk[:, n, :], parts[:, n, 0, :], ALU.subtract)
                dve.drain()
                nc.vector.tensor_copy(parts[:, n, 1, :], qk[:, n, :])
                dve.drain()
                nc.vector.tensor_tensor(parts[:, n, 2, :], qk[:, n, :], parts[:, n, 1, :], ALU.subtract).then_inc(parts_ready, 1)
                dve.drain()

            def copy_o(b, g):
                dve.wait_ge(pv_done, b * SETS + 4 * g + 4 + 16)
                dve.wait_ge(nd_done, b)
                nc.vector.tensor_copy(o_sb[:, g, :], ps_o[:, :]).then_inc(o_copied, 1)

            def weigh(b, e):
                if e == 0:
                    dve.wait_ge(cw_loaded, b * 32 + 32)
                dve.wait_ge(xe_used, b * 8 + e)
                nc.vector.tensor_tensor(xe[:, e % 2, :], xn[:, at(b)], cwb[:, e, :], ALU.mult).then_inc(xe_ready, 1)

            def normalise(b):
                dve.wait_ge(nd_done, b + 1)
                nc.vector.reciprocal(rden[:, :], ps_d[:, :])
                dve.drain()
                dve.wait_ge(y_done, b)
                nc.vector.tensor_tensor(on[:, :], ps_m[:, :], rden[:, :], ALU.mult).then_inc(on_ready, 1)

            def add(b):
                dve.wait_ge(y_done, b + 1)
                nc.vector.scalar_tensor_tensor(x[:, at(b)], ps_y[:, :], w["bproj0"], x[:, at(b)],
                                               ALU.add, ALU.add).then_inc(x_added, 1)

            def route():
                probabilities(nc, dve, lg, stat, exp_in, exp_out, E0)
                precedence(nc, dve, lg, first, E0)
                nc.vector.reduce_sum(rank[:, :, :], first[:, :, :, :], AX_X)
                dve.drain()
                nc.vector.tensor_scalar(rank[:, :, :], rank[:, :, :], 1.5, None, ALU.is_lt)
                dve.drain()
                nc.vector.tensor_tensor(cw[:, :, :], lg[:, :, 0:E0_TRUE], rank[:, :, 0:E0_TRUE], ALU.mult)
                dve.drain()
                nc.vector.reduce_sum(stat[:, 0:NT], cw[:, :, :], AX_X)
                dve.drain()
                nc.vector.tensor_scalar(stat[:, NT:2 * NT], stat[:, 0:NT], 0.0, None, ALU.is_le)
                dve.drain()
                nc.vector.tensor_tensor(stat[:, 0:NT], stat[:, 0:NT], stat[:, NT:2 * NT], ALU.add)
                dve.drain()
                nc.vector.reciprocal(stat[:, 2 * NT:3 * NT], stat[:, 0:NT])
                dve.drain()
                nc.vector.tensor_tensor(cw[:, :, :], cw[:, :, :], over(stat[:, 2 * NT:3 * NT], E0_TRUE),
                                        ALU.mult).then_inc(combined, 1)

            def attend_first():
                read(1, 0)
                copy_o(0, 0)
                read(1, 1)
                read_v(1, 1)
                dve.wait_ge(turned, 1)
                nc.vector.tensor_copy(cw_rows[:, :, :], ps_y[:, 0:2 * P].rearrange("p (k c) -> p k c", k=2)).then_inc(cw_ready, 1)
                weigh(0, 0)
                weigh(0, 1)
                copy_o(0, 1)
                weigh(0, 2)
                weigh(0, 3)
                split(1, 0)
                weigh(0, 4)
                copy_o(0, 2)
                weigh(0, 5)
                weigh(0, 6)
                split(1, 1)
                weigh(0, 7)
                copy_o(0, 3)

            def attend(b, prev, nxt, buf):
                if prev is not None:
                    normalise(prev)
                    add(prev)
                if nxt is not None:
                    read(nxt, 0)
                weigh(b, 0)
                weigh(b, 1)
                weigh(b, 2)
                copy_o(b, 0)
                if nxt is not None:
                    read(nxt, 1)
                weigh(b, 3)
                if nxt is not None:
                    read_v(nxt, 1 - buf)
                weigh(b, 4)
                weigh(b, 5)
                copy_o(b, 1)
                if nxt is not None:
                    split(nxt, 0)
                weigh(b, 6)
                weigh(b, 7)
                if nxt is not None:
                    split(nxt, 1)
                copy_o(b, 2)
                copy_o(b, 3)

            read(0, 0)
            read(0, 1)
            read_v(0, 0)
            for t in (q_stack[0], k_stack[0]):
                nc.vector.memset(t[:, :, :].bitcast(F32), 0.0).then_inc(filled, 1)
            split(0, 0)
            split(0, 1)
            route()
            attend_first()
            with dve.Fori(1, B - 1, 2) as b:
                for k in range(2):
                    attend(b + k, b + k - 1, b + k + 1, 1 - k)
            attend(B - 1, B - 2, None, 1)
            normalise(B - 1)
            add(B - 1)

        @block.tensor
        def _(pe):
            pe.sem_inc(pv_done, 16)
            pe.sem_inc(xe_used, 1)

            def project(b, n):
                if n == 0:
                    pe.wait_ge(xst_ready, b + 1)
                    pe.wait_ge(ms_read, b * 2)
                    pe.wait_ge(on_ready, b)
                else:
                    pe.wait_ge(misc_read, b * 3 + n)
                nc.tensor.matmul(ps_m[:, :], w["wq0" if n == 0 else "wk0"], xst[:, :], start=True, stop=True).then_inc(misc_done, 1)

            def project_v(b):
                pe.wait_ge(misc_read, b * 3 + 2)
                for m in range(NBLK):
                    last = nc.tensor.matmul(ps_m[:, m * P:(m + 1) * P], xst[:, m * P:(m + 1) * P], w["wv0"],
                                            start=True, stop=True)
                last.then_inc(misc_done, 1)

            def mean_square(b, n):
                pe.wait_ge(squared, b * 2 + n + 1)
                if n == 0:
                    pe.wait_ge(misc_read, b * 3 + 3)
                else:
                    pe.wait_ge(ms_read, b * 2 + 1)
                nc.tensor.matmul(ps_m[:, :], sh["common"]["mean_head"], sq[:, n, :], start=True, stop=True).then_inc(misc_done, 1)

            def scores(b, buf, s):
                g, m = s // 4, s % 4
                if s == 0:
                    pe.wait_ge(stack_ready, b * 96 + 96)
                for half in range(2):
                    u = 2 * s + half
                    pe.wait_ge(exped, b * 32 + u)
                    for j in (2 * half, 2 * half + 1):
                        h = 4 * g + j
                        last = nc.tensor.matmul(ps_s[:, j, :], k_stack[buf][:, h, m * P:(m + 1) * P],
                                                q_stack[buf][:, h, :], start=True, stop=True)
                    last.then_inc(scored, 1)

            def times_v(b, buf, s):
                g, m = s // 4, s % 4
                pe.wait_ge(exped, b * 32 + 2 * s + 3)
                if m == 0:
                    pe.wait_ge(o_copied, b * 4 + g + 1)
                for j in range(4):
                    last = nc.tensor.matmul(ps_o[32 * j:32 * j + 32, :], v[buf][:, m, 4 * g + j, :], probs[s % 2][:, j, :],
                                            start=(m == 0), stop=(m == NBLK - 1))
                last.then_inc(pv_done, 1)

            def place(b):
                pe.wait_ge(o_copied, b * 4 + 5)
                for to, name in ((ps_m, "place_num"), (ps_d, "place_den")):
                    for g in range(4):
                        last = nc.tensor.matmul(to[:, :], w[name][:, g * P:(g + 1) * P], o_sb[:, g, :],
                                                start=(g == 0), stop=(g == 3))
                last.then_inc(nd_done, 1)

            def expert(b, e):
                if e == 0:
                    pe.wait_ge(x_added, b)
                pe.wait_ge(xe_ready, b * 8 + e + 1)
                nc.tensor.matmul(ps_y[:, :], w["expert0"][:, e * P:(e + 1) * P], xe[:, e % 2, :],
                                 start=(e == 0), stop=False).then_inc(xe_used, 1)

            def expert_bias(b):
                pe.wait_ge(cw_loaded, b * 32 + 32)
                nc.tensor.matmul(ps_y[:, :], w["expert0_b"][0:E0_TRUE, :], cwT[:, :], start=False, stop=False).then_inc(biased, 1)

            def output(b):
                pe.wait_ge(on_ready, b + 2)
                nc.tensor.matmul(ps_y[:, :], w["wproj0"], on[:, :], start=False, stop=True).then_inc(y_done, 1)

            def attend(b, buf, prev, nxt):
                for s in range(SETS):
                    scores(b, buf, s)
                    if s == 0 and prev is not None:
                        pe.wait_ge(ms_read, b * 2 + 2)
                        place(prev)
                    if s == 3 and prev is not None:
                        output(prev)
                    if nxt is not None:
                        if s == 3:
                            project(nxt, 0)
                        if s == 5:
                            project(nxt, 1)
                        if s == 6:
                            project_v(nxt)
                        if s == 7:
                            mean_square(nxt, 0)
                        if s == 9:
                            mean_square(nxt, 1)
                    if prev is None and s == 3:
                        pe.wait_ge(combined, 1)
                        for k in range(2):
                            last = nc.tensor.transpose(ps_y[:, k * P:(k + 1) * P],
                                                       cw[:, :, :].rearrange("p (k t) e -> p k (t e)", k=2)[:, k, :],
                                                       sh["common"]["ident"])
                        last.then_inc(turned, 1)
                    e = s - (8 if prev is None else 4)
                    if 0 <= e < E0_TRUE:
                        if prev is None and e == 0:
                            pe.wait_ge(cw_ready, 1)
                        expert(b, e)
                    if s == (15 if prev is None else 13):
                        expert_bias(b)
                    if s > 0:
                        times_v(b, buf, s - 1)
                times_v(b, buf, SETS - 1)

            project(0, 0)
            project(0, 1)
            project_v(0)
            mean_square(0, 0)
            mean_square(0, 1)
            pe.wait_ge(filled, 6)
            attend(0, 0, None, 1)
            pe.wait_ge(filled1, 2)
            with pe.Fori(1, B - 1, 2) as b:
                for k in range(2):
                    attend(b + k, 1 - k, b + k - 1, b + k + 1)
            attend(B - 1, 1, B - 2, None)
            pe.wait_ge(x_added, B - 1)
            place(B - 1)
            output(B - 1)


WAYS1 = 8
STEPS1 = 9


def layer1_norm_and_route(nc, sh):
    xn, w = sh["xn"], sh["w"][1]
    with ExitStack() as ctx:
        sb = lambda name, shape, dt=F32: ctx.enter_context(nc.sbuf_tensor(name, shape, dt))
        sem = lambda name: ctx.enter_context(nc.semaphore(name))
        xc = sb("n1_xc", [P, NTOK])
        pr = sb("n1_prob", [P, NT, E1])
        first = sb("n1_first", [P, NT, E1, E1])
        tie = sb("n1_tie", [P, NT, E1, E1])
        rank = sb("n1_rank", [P, NT, E1])
        mass = sb("n1_mass", [P, NT, E1])
        stat = sb("n1_stat", [P, 3 * NT])
        prk = sb("n1_prk", [P, 2, E1, 16])
        rkk = sb("n1_rkk", [P, 2, E1, 16])
        prT = sb("n1_prT", [P, 2 * P])
        rkT = sb("n1_rkT", [P, 2 * P])
        ge = sb("n1_ge", [P, 2 * P])
        eq = sb("n1_eq", [P, 2 * P])
        cum = sh["score_rows"]
        ones = sb("n1_ones", [P, 2 * P])
        s = sb("n1_small", [P, 4])
        compared = first[:, :, :, :].rearrange("p t e f -> p (t e f)")
        thr, step, moves, above = (s[:, i:i + 1] for i in range(4))
        cand, cnt, passed = (sb(f"n1_{n}", [P, WAYS1 - 1]) for n in ("cand", "count", "passed"))
        ps = ctx.enter_context(nc.psum_tensor("n1_ps", [P, 8, 512], F32))
        logits_done, exp_in, exp_out, ranked, turned, counted, summed, prefix_done, scored = (
            sem(n) for n in ("r_logits_done", "r_exp_in", "r_exp_out", "ranked", "r_turned", "counted",
                             "summed", "prefix_done", "scored1"))
        high_ready, low_ready = sem("high_ready"), sem("low_ready")
        lnd, lnd_row, d_o, d_v, d_chunk = (sh["decay"][n] for n in ("lnd", "lnd_row", "d_o", "d_v", "d_chunk"))
        ln_pe, ln_dve, ln_act, normed = layer_norm(nc, ctx, sh, xc, ps)
        block = ctx.enter_context(nc.Block())

        @block.sync
        def _(sp):
            for n in (1, 2, 3):
                sp.dma_start(sh["w"][n].tensor[:, :], sh["w_dram"][n]).then_inc(sh["w_loaded"][n], 16)
            sp.wait_ge(scored, 1)
            sp.dma_start(sh["score_dram"].rearrange("e (g f) -> (e g) f", g=16), cum[:, :]).then_inc(sh["scores_stored"], 16)

        @block.tensor
        def _(pe):
            ln_pe(pe)
            pe.wait_ge(sh["w_loaded"][1], 16)
            gate_logits(nc, pe, xn, w["gate1"], ps, E1, normed, logits_done)
            pe.wait_ge(ranked, 1)
            for i, a in enumerate((prk, rkk)):
                for k in range(2):
                    last = nc.tensor.transpose(ps[:, 1, (2 * i + k) * P:(2 * i + k + 1) * P],
                                               a[:, k, :, :].rearrange("p e g -> p (e g)"), sh["common"]["ident"])
            last.then_inc(turned, 1)
            with pe.Fori(0, STEPS1) as i:
                pe.wait_ge(counted, i + 1)
                nc.tensor.matmul(ps[:, 2, 0:WAYS1 - 1], w["sum_expert"], cnt[:, :], start=True, stop=True).then_inc(summed, 1)
            pe.wait_ge(counted, STEPS1 + 1)
            nc.tensor.matmul(ps[:, 2, 0:1], w["sum_expert"], above, start=True, stop=False)
            nc.tensor.matmul(ps[:, 2, 0:1], w["before_group"], cum[:, 2 * P - 1:2 * P], start=False, stop=True).then_inc(prefix_done, 1)

        @block.scalar
        def _(act):
            nc.scalar.preload_act_table_set("natural_log_exp_and_others")
            ln_act(act)
            act.wait_ge(exp_in, 1)
            nc.scalar.activation(pr[:, :, :], pr[:, :, :], ACT.Exp).then_inc(exp_out, 1)
            nc.scalar.activation(lnd[:, :], w["decay_col"], ACT.Exp, scale=-1.0)
            nc.scalar.activation(lnd_row[:, :], w["decay_row"], ACT.Exp, scale=-1.0)
            act.drain()
            nc.scalar.activation(lnd[:, :], lnd[:, :], ACT.Ln, bias=sh["eps"][:, 1:2])
            nc.scalar.activation(lnd_row[:, :], lnd_row[:, :], ACT.Ln, bias=sh["eps"][:, 1:2])
            act.drain()
            nc.scalar.mul(lnd[:, :], lnd[:, :], -1.0)
            nc.scalar.mul(lnd_row[:, :], lnd_row[:, :], -1.0)
            act.drain()
            nc.scalar.activation(d_o[:, :], w["chunk_o_pow"][0:DS, :], ACT.Exp, scale=lnd[0:DS, :])
            nc.scalar.activation(d_v[:, :], lnd_row[:, :], ACT.Exp, scale=w["chunk_v_pow"])
            nc.scalar.activation(d_chunk[:, :], lnd_row[:, :], ACT.Exp, scale=float(C1))
            act.wait_ge(sh["w_loaded"][2], 16)
            nc.scalar.activation(single(sh["w2_high"].tensor[:, :]), sh["w"][2].tensor[:, :], ACT.Copy).then_inc(high_ready, 1)

        @block.gpsimd
        def _(pool):
            pool.wait_ge(high_ready, 1)
            nc.gpsimd.tensor_tensor(single(sh["w2_low"].tensor[:, :]), sh["w"][2].tensor[:, :],
                                    sh["w2_high"].tensor[:, :], ALU.subtract).then_inc(low_ready, 1)
            pool.wait_ge(low_ready, 1)

        @block.vector
        def _(dve):
            ln_dve(dve)
            dve.wait_ge(logits_done, 1)
            nc.vector.tensor_copy(pr[:, :, :], ps[:, 0, 0:NT * E1].rearrange("p (t e) -> p t e", e=E1))
            dve.drain()
            probabilities(nc, dve, pr, stat, exp_in, exp_out, E1)
            precedence(nc, dve, pr, first, E1)
            nc.vector.reduce_sum(rank[:, :, :], first[:, :, :, :], AX_X)
            nc.vector.tensor_tensor(tie[:, :, :, :], first[:, :, :, :],
                                    pr[:, :, :].unsqueeze(2).broadcast_to([P, NT, E1, E1]), ALU.mult)
            dve.drain()
            nc.vector.reduce_sum(mass[:, :, :], tie[:, :, :, :], AX_X)
            dve.drain()
            nc.vector.tensor_scalar(mass[:, :, :], mass[:, :, :], 0.9, None, ALU.is_lt)
            nc.vector.tensor_scalar(rank[:, :, :], rank[:, :, :], 1.0, None, ALU.add)
            dve.drain()
            nc.vector.tensor_tensor(rank[:, :, :], pr[:, :, :], rank[:, :, :], ALU.subtract)
            dve.drain()
            nc.vector.tensor_tensor(rank[:, :, :], rank[:, :, :], mass[:, :, :], ALU.mult)
            dve.drain()
            nc.vector.tensor_scalar(mass[:, :, :], mass[:, :, :], 1.0, 1e9, ALU.subtract, ALU.mult)
            dve.drain()
            nc.vector.tensor_tensor(rkk[:, :, :, :].rearrange("p k e g -> p g k e"),
                                    rank[:, :, :].rearrange("p (g k) e -> p g k e", k=2),
                                    mass[:, :, :].rearrange("p (g k) e -> p g k e", k=2), ALU.add)
            nc.vector.tensor_copy(prk[:, :, :, :].rearrange("p k e g -> p g k e"),
                                  pr[:, :, :].rearrange("p (g k) e -> p g k e", k=2))
            dve.drain()
            nc.vector.memset(ones[:, :], 1.0).then_inc(ranked, 1)
            nc.vector.memset(thr, -8.0)
            nc.vector.memset(step, 8.0 / WAYS1)
            dve.wait_ge(turned, 1)
            nc.vector.tensor_copy(prT[:, :], ps[:, 1, 0:2 * P])
            nc.vector.tensor_copy(rkT[:, :], ps[:, 1, 2 * P:4 * P])
            dve.drain()
            with dve.Fori(0, STEPS1) as i:
                nc.vector.tensor_scalar(cand[:, :], w["ways"], step, thr, ALU.mult, ALU.add)
                dve.drain()
                for c in range(WAYS1 - 1):
                    last = nc.vector.tensor_scalar(compared[:, c * 2 * P:(c + 1) * 2 * P], rkT[:, :], cand[:, c:c + 1], None,
                                                   ALU.is_ge, ALU.add, accum_out=cnt[:, c:c + 1])
                last.then_inc(counted, 1)
                dve.wait_ge(summed, i + 1)
                nc.vector.tensor_scalar(passed[:, :], ps[:, 2, 0:WAYS1 - 1], CAP - 0.5, None, ALU.is_ge, ALU.add, accum_out=moves)
                dve.drain()
                nc.vector.scalar_tensor_tensor(thr, moves, step, thr, ALU.mult, ALU.add)
                dve.drain()
                nc.vector.tensor_scalar(step, step, 1.0 / WAYS1, None, ALU.mult)
                dve.drain()
            nc.vector.tensor_scalar(ge[:, :], rkT[:, :], thr, None, ALU.is_gt, ALU.add, accum_out=above)
            nc.vector.tensor_scalar(eq[:, :], rkT[:, :], thr, None, ALU.is_equal)
            dve.drain()
            nc.vector.tensor_tensor_scan(cum[:, :], ones[:, :], eq[:, :], 0.0, ALU.mult, ALU.add).then_inc(counted, 1)
            dve.wait_ge(prefix_done, 1)
            nc.vector.tensor_scalar(cum[:, :], cum[:, :], ps[:, 2, 0:1], CAP + 0.5, ALU.add, ALU.is_lt)
            dve.drain()
            nc.vector.tensor_tensor(cum[:, :], cum[:, :], eq[:, :], ALU.mult)
            dve.drain()
            nc.vector.tensor_tensor(cum[:, :], cum[:, :], ge[:, :], ALU.add)
            dve.drain()
            nc.vector.tensor_tensor(cum[:, :], cum[:, :], prT[:, :], ALU.mult).then_inc(scored, 1)


def layer1_mix(nc, sh):
    x, xn, w = sh["x"], sh["xn"], sh["w"][1]
    with ExitStack() as ctx:
        sb = lambda name, shape, dt=F32: ctx.enter_context(nc.sbuf_tensor(name, shape, dt))
        sem = lambda name: ctx.enter_context(nc.semaphore(name))
        d_o, d_v, d_chunk = (sh["decay"][n] for n in ("d_o", "d_v", "d_chunk"))
        xst = sb("xst1", [P, T])
        q, k = sb("q1", [DS, T]), sb("k1", [DS, T])
        kv = sb("kv1", [P, NBLK, 2 * DS])
        v_chunk = sb("v_chunk", [P, NBLK, P // C1, DS])
        inside = sb("inside", [P, NBLK, P])
        state = sb("state1", [DS, NC1, DS])
        o = sb("o1", [P, T])
        score = [sb(f"score{i}", [P, E1, T]) for i in range(2)]
        h = sb("h1", [P, 2, T])
        hs = sb("hs1", [P, 2, T])
        ps_q = ctx.enter_context(nc.psum_tensor("ps_q1", [P, 512], F32))
        ps_k = ctx.enter_context(nc.psum_tensor("ps_k1", [P, 512], F32))
        ps_kv = ctx.enter_context(nc.psum_tensor("ps_kv1", [P, 512], F32))
        ps_a = ctx.enter_context(nc.psum_tensor("ps_a1", [P, 512], F32))
        ps_u = ctx.enter_context(nc.psum_tensor("ps_u1", [P, 512], F32))
        ps_h = ctx.enter_context(nc.psum_tensor("ps_h1", [P, 2, 512], F32))
        ps_y = ctx.enter_context(nc.psum_tensor("ps_y1", [P, 512], F32))

        staged = sem("staged1")
        proj_done = sem("proj_done1")
        proj_read = sem("proj_read1")
        a_done, a_read = sem("a_done"), sem("a_read")
        u_done, s_ready = sem("u_done"), sem("s_ready")
        o_done, o_read = sem("o_done"), sem("o_read")
        up_done = sem("up_done")
        h_ready = sem("h_ready")
        hs_ready = sem("hs_ready")
        down_done = sem("down_done")
        y_done, x_added = sem("y_done1"), sem("x_added1")
        score_loaded = [sem("score_loaded0"), sem("score_loaded1")]
        o_zero = sem("o_zero")
        block = ctx.enter_context(nc.Block())

        @block.sync
        def _(sp):
            sp.wait_ge(sh["scores_stored"], 16)
            with sp.Fori(0, B // 2) as i:
                for j in range(2):
                    start = sp.snap(i * (2 * T) + j * T)
                    sp.wait_ge(x_added, i * 2 + j)
                    sp.dma_start(score[j][:, :, :], sh["score_dram"][:, bass.ds(start, T)].unsqueeze(0).broadcast_to([P, E1, T])
                                 ).then_inc(score_loaded[j], 16)

        @block.gpsimd
        def _(pool):
            def stage(b):
                nc.gpsimd.tensor_copy(xst[:, :], xn[:, at(b)]).then_inc(staged, 1)

            stage(0)
            nc.gpsimd.memset(o[:, :], 0.0).then_inc(o_zero, 1)
            with pool.Fori(1, B) as b:
                pool.wait_ge(proj_done, b * 3)
                stage(b)

        @block.scalar
        def _(act):
            act.sem_inc(h_ready, 1)
            with act.Fori(0, B) as b:
                for e in range(E1):
                    act.wait_ge(up_done, b * E1 + e + 1)
                    act.wait_ge(hs_ready, b * E1 + e)
                    nc.scalar.activation(h[:, e % 2, :], ps_h[:, e % 2, :], ACT.Gelu).then_inc(h_ready, 1)

        @block.vector
        def _(dve):
            dve.sem_inc(hs_ready, 1)
            dve.sem_inc(x_added, 1)

            def weigh(b, buf, e):
                if e == 0:
                    dve.wait_ge(score_loaded[buf], (b - buf) * 8 + 16)
                dve.wait_ge(h_ready, b * E1 + e + 2)
                dve.wait_ge(down_done, b * E1 + e)
                nc.vector.tensor_tensor(hs[:, e % 2, :], h[:, e % 2, :], score[buf][:, e, :], ALU.mult).then_inc(hs_ready, 1)

            def powers(table, n, m):
                return table.unsqueeze(1).broadcast_to([table.shape[0], n, m])

            def batch(b, buf):
                for n, (to, ps, bias) in enumerate(((q, ps_q, "bq1"), (k, ps_k, "bk1"))):
                    dve.wait_ge(proj_done, b * 3 + n + 1)
                    nc.vector.tensor_scalar(to[:, :], ps[0:DS, :], w[bias][0:DS, :], None, ALU.add).then_inc(proj_read, 1)
                dve.wait_ge(proj_done, b * 3 + 3)
                nc.vector.tensor_tensor(kv[:, :, :], ps_kv[:, :].rearrange("p (m c) -> p m c", m=NBLK),
                                        powers(w["bkv1"], NBLK, 2 * DS), ALU.add)
                dve.drain()
                nc.vector.tensor_tensor(kv[:, :, DS:2 * DS], kv[:, :, DS:2 * DS], powers(d_v[:, :], NBLK, DS), ALU.mult)
                dve.drain()
                chunks = [P, NBLK, P // C1, DS]
                nc.vector.tensor_tensor(v_chunk[:, :, :, :], kv[:, :, DS:2 * DS].unsqueeze(2).broadcast_to(chunks),
                                        w["chunk_of"].unsqueeze(1).unsqueeze(3).broadcast_to(chunks), ALU.mult).then_inc(proj_read, 1)
                weigh(b, buf, 0)
                dve.wait_ge(a_done, b + 1)
                nc.vector.tensor_tensor(inside[:, :, :], ps_a[:, :].rearrange("p (m t) -> p m t", m=NBLK),
                                        powers(w["causal"], NBLK, P), ALU.mult).then_inc(a_read, 1)
                weigh(b, buf, 1)
                dve.wait_ge(u_done, b + 1)
                nc.vector.tensor_copy(state[:, 1, :], ps_u[0:DS, 0:DS])
                for c in range(1, NC1):
                    if c > 1:
                        nc.vector.tensor_tensor(state[:, c, :], state[:, c - 1, :], ps_u[0:DS, (c - 1) * DS:c * DS], ALU.add)
                    dve.drain()
                    last = nc.vector.tensor_tensor(state[:, c, :], state[:, c, :], d_chunk[0:DS, :], ALU.mult)
                    if c < NC1 - 1:
                        dve.drain()
                last.then_inc(s_ready, 1)
                weigh(b, buf, 2)
                weigh(b, buf, 3)
                dve.wait_ge(o_done, b + 1)
                dve.wait_ge(o_zero, 1)
                dve.wait_ge(y_done, b)
                nc.vector.tensor_tensor(o[0:DS, :].rearrange("p (c t) -> p c t", t=C1),
                                        ps_q[0:DS, :].rearrange("p (c t) -> p c t", t=C1),
                                        powers(d_o[:, :], NC1, C1), ALU.mult).then_inc(o_read, 1)
                for e in range(4, E1):
                    weigh(b, buf, e)
                nc.vector.tensor_tensor(x[:, at(b)], x[:, at(b)], xn[:, at(b)], ALU.add)
                dve.drain()
                dve.wait_ge(y_done, b + 1)
                nc.vector.scalar_tensor_tensor(x[:, at(b)], ps_y[:, :], w["bo1"], x[:, at(b)],
                                               ALU.add, ALU.add).then_inc(x_added, 1)

            with dve.Fori(0, B // 2) as i:
                for j in range(2):
                    batch(i * 2 + j, j)

        @block.tensor
        def _(pe):
            pe.sem_inc(down_done, 1)

            def up(b, e):
                pe.wait_ge(h_ready, b * E1 + e)
                nc.tensor.matmul(ps_h[:, e % 2, :], w["up1"][:, e * F1:(e + 1) * F1], xn[:, at(b)], start=True, stop=True).then_inc(up_done, 1)

            def down(b, e):
                if e == 0:
                    pe.wait_ge(x_added, b + 1)
                pe.wait_ge(hs_ready, b * E1 + e + 2)
                nc.tensor.matmul(ps_y[:, :], w["down1"][:, e * P:(e + 1) * P], hs[:, e % 2, :],
                                 start=(e == 0), stop=False).then_inc(down_done, 1)

            with pe.Fori(0, B) as b:
                pe.wait_ge(staged, b + 1)
                pe.wait_ge(o_read, b)
                nc.tensor.matmul(ps_q[0:DS, :], w["wq1"], xst[:, :], start=True, stop=True).then_inc(proj_done, 1)
                nc.tensor.matmul(ps_k[0:DS, :], w["wk1"], xst[:, :], start=True, stop=True).then_inc(proj_done, 1)
                for m in range(NBLK):
                    last = nc.tensor.matmul(ps_kv[:, m * P:(m + 1) * P], xst[:, m * P:(m + 1) * P], w["wkv1"],
                                            start=True, stop=True)
                last.then_inc(proj_done, 1)
                up(b, 0)
                up(b, 1)
                pe.wait_ge(proj_read, b * 3 + 2)
                pe.wait_ge(a_read, b)
                for m in range(NBLK):
                    last = nc.tensor.matmul(ps_a[:, m * P:(m + 1) * P], k[:, m * P:(m + 1) * P], q[:, m * P:(m + 1) * P],
                                            start=True, stop=True)
                last.then_inc(a_done, 1)
                pe.wait_ge(proj_read, b * 3 + 3)
                pe.wait_ge(s_ready, b)
                for m in range(NBLK):
                    last = nc.tensor.matmul(ps_u[0:DS, m * P:(m + 1) * P], kv[:, m, 0:DS],
                                            v_chunk[:, m, :, :].rearrange("p c i -> p (c i)"), start=True, stop=True)
                last.then_inc(u_done, 1)
                down(b, 0)
                up(b, 2)
                down(b, 1)
                up(b, 3)
                pe.wait_ge(a_read, b + 1)
                pe.wait_ge(s_ready, b + 1)
                for m in range(NBLK):
                    nc.tensor.matmul(ps_q[0:DS, m * P:(m + 1) * P], kv[:, m, DS:2 * DS], inside[:, m, :],
                                     start=True, stop=False)
                    for c in range(2 * m, 2 * m + 2):
                        if c:
                            last = nc.tensor.matmul(ps_q[0:DS, c * C1:(c + 1) * C1], state[:, c, :],
                                                    q[:, c * C1:(c + 1) * C1], start=False, stop=(c % 2 == 1))
                last.then_inc(o_done, 1)
                for e in range(2, E1):
                    down(b, e)
                    if e + 2 < E1:
                        up(b, e + 2)
                pe.wait_ge(o_zero, 1)
                pe.wait_ge(o_read, b + 1)
                nc.tensor.matmul(ps_y[:, :], w["wo1"], o[:, :], start=False, stop=True).then_inc(y_done, 1)


def norm_only(nc, sh, name, load=None):
    with ExitStack() as ctx:
        xc = ctx.enter_context(nc.sbuf_tensor(f"{name}_xc", [P, NTOK], F32))
        ps = ctx.enter_context(nc.psum_tensor(f"{name}_ps", [P, 8, 512], F32))
        ln_pe, ln_dve, ln_act, _ = layer_norm(nc, ctx, sh, xc, ps)
        block = ctx.enter_context(nc.Block())

        @block.sync
        def _(sp):
            if load is not None:
                sp.dma_start(sh["w"][load].tensor[:, :], sh["w_dram"][load]).then_inc(sh["w_loaded"][load], 16)

        @block.tensor
        def _(pe):
            ln_pe(pe)

        @block.vector
        def _(dve):
            ln_dve(dve)

        @block.scalar
        def _(act):
            nc.scalar.preload_act_table_set("natural_log_exp_and_others")
            ln_act(act)


USE_Q, USE_K, USE_GATE, USE_V, USE_H1, USE_H2, USE_S = (0, 1), (2, 3), (4, 5, 6, 7), (8, 9, 12, 13), (10, 11), (14, 15), 16
WIDE = 16


def split_products(nc, out, a, b, start=True, stop=True):
    terms = ((a[1], b[0]), (a[0], b[1]), (a[0], b[0]))
    for n, (lhsT, rhs) in enumerate(terms):
        last = nc.tensor.matmul(out, single(lhsT), single(rhs), start=(start and n == 0), stop=(stop and n == 2))
    return last


def layer2_mix(nc, sh):
    x, xn, w, wh, wl = sh["x"], sh["xn"], sh["w"][3], sh["w2_high"], sh["w2_low"]
    ident = sh["common"]["ident"]
    with ExitStack() as ctx:
        sb = lambda name, shape, dt=F32: ctx.enter_context(nc.sbuf_tensor(name, shape, dt))
        sem = lambda name: ctx.enter_context(nc.semaphore(name))
        xh, xl = sb("xh2", [P, T]), sb("xl2", [P, T])
        qq = sb("qq2", [P, H2, T])
        ql = sb("ql2", [P, H2, T])
        kk = sb("kk2", [P, H2, T])
        kh = sb("kh2", [P, 2, T])
        v = sb("v2", [P, NBLK, H2, D + 1])
        probs = sb("probs2", [P, 2, NBLK, T])
        by_head = probs[:, :, :, :].rearrange("p a m t -> p (a m) t")
        raw = sb("raw2", [P, 2, T])
        gate_high, gate_low = sb("gate_high2", [P, FT, T]), sb("gate_low2", [P, FT, T])
        hidden = {"h1_2": by_head[:, FT:2 * FT, :], "h2_2": by_head[:, 0:FT, :]}
        no_rows = sb("no_rows2", [P, 2])
        top = sb("max2", [P, H2, NBLK])
        topT = sb("maxT2", [H2 * NBLK, P])
        rden = sb("rden2", [P, 2, NBLK])
        att = sb("att2", [P, NBLK, D])
        ps_w = [ctx.enter_context(nc.psum_tensor(f"ps_wide{i}", [P, 2, 512], F32)) for i in range(2)]
        ps_o = [ctx.enter_context(nc.psum_tensor(f"ps_o2_{i}", [P, 2, 512], F32)) for i in range(2)]

        pads = sem("pads2")
        xh_ready, x_split = sem("xh_ready2"), sem("x_split2")
        wide_done = [sem("wide_done0"), sem("wide_done1")]
        wide_read = [sem("wide_read0"), sem("wide_read1")]
        qh_ready = sem("qh_ready2")
        qq_ready = sem("qq_ready2")
        kk4_ready = sem("kk4_ready2")
        lows_ready = sem("lows_ready2")
        kh_ready = sem("kh_ready2")
        gated = sem("gated2")
        split = sem("split2")
        max_done, max_read = sem("max_done2"), sem("max_read2")
        maxT_done, maxT_read = sem("maxT_done2"), sem("maxT_read2")
        shifted = sem("shifted2")
        y_done, y_added = sem("y_done2"), sem("y_added2")
        o_done, o_read = sem("o_done2"), sem("o_read2")
        att_done, att_added = sem("att_done2"), sem("att_added2")
        block = ctx.enter_context(nc.Block())

        def filled(eng, b, use):
            eng.wait_ge(wide_done[use % 2], b * WIDE + use // 2 + 1)

        def was_read(eng, b, use):
            eng.wait_ge(wide_read[use % 2], b * WIDE + use // 2 + 1)

        @block.gpsimd
        def _(pool):
            def x_low(b):
                pool.wait_ge(xh_ready, b + 1)
                nc.gpsimd.tensor_tensor(single(xl[:, :]), xn[:, at(b)], xh[:, :], ALU.subtract).then_inc(x_split, 1)

            def batch(b, following):
                pool.wait_ge(qh_ready, 2 * b + 2)
                for first, is_k in ((4, False), (0, True), (0, False)):
                    heads = slice(first, first + 4)
                    if is_k:
                        pool.wait_ge(kh_ready, b * (H2 + 1) + 1)
                        nc.gpsimd.tensor_tensor(single(kk[R2:P, heads, :]), by_head[0:R2, heads, :], kk[0:R2, heads, :],
                                                ALU.subtract).then_inc(lows_ready, 1)
                    else:
                        nc.gpsimd.tensor_tensor(single(ql[0:R2, heads, :]), by_head[R2:P, heads, :], qq[R2:P, heads, :],
                                                ALU.subtract).then_inc(lows_ready, 1)
                    pool.drain()
                pool.wait_ge(maxT_read, b + 1)
                if following is not None:
                    x_low(following)
                pool.dma_start(single(ql[R2:R2 + 1, :, :]).rearrange("o h (m t) -> o (h m) t", t=P),
                               single(topT[:, :])).then_inc(shifted, 16)

            x_low(0)
            pool.drain()
            nc.gpsimd.memset(no_rows[:, 0:1], 0.0)
            pool.drain()
            nc.gpsimd.memset(no_rows[:, 1:2], 1.0)
            pool.drain()
            nc.gpsimd.tensor_copy(single(ql[R2:P, :, :]), no_rows[R2:P, 0:1].unsqueeze(2).broadcast_to([R2, H2, T]))
            pool.drain()
            nc.gpsimd.tensor_copy(single(kh[R2:P, :, :]), no_rows[R2:P, 0:1].unsqueeze(2).broadcast_to([R2, 2, T]))
            pool.drain()
            nc.gpsimd.tensor_copy(single(kh[R2:R2 + 1, :, :]), no_rows[R2:R2 + 1, 1:2].unsqueeze(2).broadcast_to([1, 2, T]))
            pool.drain()
            nc.gpsimd.memset(v[:, :, :, D:D + 1], 1.0).then_inc(pads, 1)
            pool.drain()
            with pool.Fori(0, B - 1) as b:
                batch(b, b + 1)
            batch(B - 1, None)
            pool.wait_ge(shifted, B * 16)

        def take_heads(engine_copy, row, b, use, i, eng):
            filled(eng, b, use)
            h = 4 * i
            ps = ps_w[use % 2]
            engine_copy(by_head[row:row + R2, h:h + 4:2, :], ps[0:R2, :, :])
            engine_copy(by_head[row:row + R2, h + 1:h + 4:2, :], ps[R2:P, :, :]).then_inc(wide_read[use % 2], 1)

        @block.scalar
        def _(act):
            copy = lambda out, in_: nc.scalar.activation(out, in_, ACT.Copy)

            def copy_kh(h):
                copy(single(kh[0:R2, h % 2, :]), kk[0:R2, h, :]).then_inc(kh_ready, 1)

            def take_v(b, m):
                use = USE_V[m]
                filled(act, b, use)
                nc.scalar.activation(v[:, m, :, 0:D], ps_w[use % 2][:, :, :].rearrange("p a (h d) -> p (a h) d", d=D),
                                     ACT.Copy).then_inc(wide_read[use % 2], 1)

            def gelu(b, uses, name, scale):
                for i in range(2):
                    filled(act, b, uses[i])
                    for j in range(2):
                        t = 2 * i + j
                        last = nc.scalar.activation(hidden[name][:, t, :], ps_w[i][:, j, :], ACT.Gelu, scale=w[scale][:, t:t + 1])
                    last.then_inc(wide_read[i], 1)

            with act.Fori(0, B) as b:
                take_heads(copy, R2, b, USE_Q[0], 0, act)
                act.drain()
                copy(single(qq[R2:P, 0:4, :]), by_head[R2:P, 0:4, :]).then_inc(qh_ready, 1)
                take_heads(copy, 0, b, USE_K[0], 0, act)
                act.drain()
                for t in range(FT):
                    act.wait_ge(split, b * FT + t)
                    filled(act, b, USE_GATE[t])
                    nc.scalar.activation(raw[:, t % 2, :], ps_w[t % 2][:, 0, :], ACT.Silu,
                                         scale=w["s1_2"][:, t:t + 1]).then_inc(gated, 1)
                    if t == 0:
                        copy(single(kk[0:R2, 0:4, :]), by_head[0:R2, 0:4, :]).then_inc(kh_ready, 1)
                        act.wait_ge(qh_ready, 2 * b + 2)
                    copy(single(qq[0:R2, 2 * t:2 * t + 2, :]), qq[R2:P, 2 * t:2 * t + 2, :]).then_inc(qq_ready, 1)
                take_v(b, 0)
                take_v(b, 1)
                act.wait_ge(kk4_ready, b + 1)
                act.wait_ge(lows_ready, b * 3 + 1)
                gelu(b, USE_H1, "h1_2", "sh1_2")
                take_v(b, 2)
                take_v(b, 3)
                copy_kh(0)
                copy_kh(1)
                act.wait_ge(lows_ready, b * 3 + 3)
                gelu(b, USE_H2, "h2_2", "sh2_2")
                for h in range(H2):
                    for i in range(2):
                        if h >= 2:
                            act.wait_ge(o_done, b * H2 + h - 1)
                        elif h == 1:
                            act.wait_ge(y_done, b + 1)
                        filled(act, b, USE_S + 2 * h + i)
                        nc.scalar.activation(probs[:, (h + 1) % 2, 2 * i:2 * i + 2, :], ps_w[i][:, :, :], ACT.Exp).then_inc(wide_read[i], 1)
                    if h + 2 < H2:
                        copy_kh(h + 2)

        @block.vector
        def _(dve):
            dve.sem_inc(max_read, 1)
            dve.sem_inc(o_read, 1)
            dve.sem_inc(split, 1)

            def split_tile(t):
                nc.vector.tensor_copy(single(gate_high[:, t, :]), raw[:, t % 2, :])
                dve.drain()
                nc.vector.tensor_tensor(single(gate_low[:, t, :]), raw[:, t % 2, :], gate_high[:, t, :], ALU.subtract).then_inc(split, 1)

            def maximum(b, u):
                dve.wait_ge(max_done, b * H2 * NBLK + u + 1)
                nc.vector.reduce_max(top[:, u // NBLK, u % NBLK:u % NBLK + 1], ps_o[1][:, u % 2, :], AX_X).then_inc(max_read, 1)

            def x_high(b):
                nc.vector.tensor_copy(single(xh[:, :]), xn[:, at(b)]).then_inc(xh_ready, 1)

            def add_attention(b):
                dve.wait_ge(att_done, b + 1)
                nc.vector.tensor_tensor(x[:, at(b)], x[:, at(b)], ps_o[0][:, 0, :], ALU.add).then_inc(att_added, 1)

            def take_gate(b, t):
                dve.wait_ge(gated, b * FT + t + 1)
                nc.vector.scalar_tensor_tensor(raw[:, t % 2, :], ps_w[t % 2][:, 1, :], w["s2_2"][:, t:t + 1], raw[:, t % 2, :],
                                               ALU.mult, ALU.mult).then_inc(wide_read[t % 2], 1)

            def batch(b, last_one, following):
                take_heads(nc.vector.tensor_copy, R2, b, USE_Q[1], 1, dve)
                dve.drain()
                nc.vector.tensor_copy(single(qq[R2:P, 4:H2, :]), by_head[R2:P, 4:H2, :]).then_inc(qh_ready, 1)
                take_heads(nc.vector.tensor_copy, 0, b, USE_K[1], 1, dve)
                dve.drain()
                for t in range(FT):
                    take_gate(b, t)
                    dve.drain()
                    split_tile(t)
                    if t == 0:
                        nc.vector.tensor_copy(single(kk[0:R2, 4:H2, :]), by_head[0:R2, 4:H2, :])
                    if t == 3:
                        nc.vector.tensor_tensor(single(kk[R2:P, 4:H2, :]), by_head[0:R2, 4:H2, :], kk[0:R2, 4:H2, :],
                                                ALU.subtract).then_inc(kk4_ready, 1)
                if last_one is not None:
                    add_attention(last_one)
                for u in range(H2 * NBLK):
                    maximum(b, u)
                dve.wait_ge(maxT_done, b + 1)
                nc.vector.tensor_scalar(single(topT[:, :]), ps_o[0][0:H2 * NBLK, 1, 0:P], -1.0, None, ALU.mult).then_inc(maxT_read, 1)
                if following is not None:
                    x_high(following)
                dve.wait_ge(y_done, b + 1)
                nc.vector.scalar_tensor_tensor(x[:, at(b)], ps_o[0][:, 0, :], w["s3_2"], x[:, at(b)],
                                               ALU.mult, ALU.add).then_inc(y_added, 1)
                for h in range(H2):
                    ps = ps_o[h % 2]
                    dve.wait_ge(o_done, b * H2 + h + 1)
                    for half in range(2):
                        nc.vector.reciprocal(rden[:, h % 2, 2 * half:2 * half + 2],
                                             ps[:, half, 0:2 * (D + 1)].rearrange("p (m d) -> p m d", d=D + 1)[:, :, D])
                    dve.drain()
                    for m in range(NBLK):
                        o = ps[:, m // 2, (m % 2) * (D + 1):(m % 2) * (D + 1) + D]
                        r = rden[:, h % 2, m:m + 1]
                        if h == 0:
                            last = nc.vector.tensor_scalar(att[:, m, :], o, r, None, ALU.mult)
                        else:
                            last = nc.vector.scalar_tensor_tensor(att[:, m, :], o, r, att[:, m, :], ALU.mult, ALU.add)
                    last.then_inc(o_read, 1)

            x_high(0)
            batch(0, None, 1)
            with dve.Fori(1, B - 1) as b:
                batch(b, b - 1, b + 1)
            batch(B - 1, B - 2, None)
            add_attention(B - 1)

        @block.tensor
        def _(pe):
            def weight(name, first, n=P):
                return wh[name][:, first:first + n], wl[name][:, first:first + n]

            def slot(b, use):
                pe.wait_ge(wide_read[use % 2], b * WIDE + use // 2)
                return ps_w[use % 2]

            def maximum(b, u):
                h, m = u // NBLK, u % NBLK
                pe.wait_ge(max_read, b * H2 * NBLK + u)
                nc.tensor.matmul(ps_o[1][:, u % 2, :], single(qq[:, h, m * P:(m + 1) * P]), single(kk[:, h, :]),
                                 start=True, stop=True).then_inc(max_done, 1)

            def scores(b, h):
                pe.wait_ge(kh_ready, b * (H2 + 1) + h + 2)
                for i in range(2):
                    ps = slot(b, USE_S + 2 * h + i)
                    for j in range(2):
                        keys = slice((2 * i + j) * P, (2 * i + j + 1) * P)
                        nc.tensor.matmul(ps[:, j, :], single(kh[:, h % 2, keys]), single(ql[:, h, :]), start=True, stop=False)
                        last = nc.tensor.matmul(ps[:, j, :], single(kk[:, h, keys]), single(qq[:, h, :]), start=False, stop=True)
                    last.then_inc(wide_done[i], 1)

            def values(b, m):
                use = USE_V[m]
                ps = slot(b, use)
                tokens = slice(m * P, (m + 1) * P)
                for j in range(2):
                    last = split_products(nc, ps[:, j, :], (xh[:, tokens], xl[:, tokens]), weight("wv2", j * T, T))
                    for u in range(8 + 4 * (m - 2) + 2 * j, 8 + 4 * (m - 2) + 2 * j + 2):
                        if m >= 2:
                            maximum(b, u)
                last.then_inc(wide_done[use % 2], 1)

            def turn_attention(b):
                pe.wait_ge(o_read, b * H2 + H2 + 1)
                for m in range(NBLK):
                    last = nc.tensor.transpose(ps_o[0][:, 0, m * P:(m + 1) * P], att[:, m, :], ident)
                last.then_inc(att_done, 1)

            def batch(b, last_one):
                here = (xh[:, :], xl[:, :])
                pe.wait_ge(x_split, b + 1)
                for uses, name in ((USE_Q, "wq2"), (USE_K, "wk2")):
                    for i, use in enumerate(uses):
                        ps = slot(b, use)
                        for j in range(2):
                            last = split_products(nc, ps[:, j, :], weight(name, (2 * i + j) * P), here)
                        last.then_inc(wide_done[i], 1)
                if last_one is not None:
                    turn_attention(last_one)
                for t in range(FT):
                    ps = slot(b, USE_GATE[t])
                    split_products(nc, ps[:, 0, :], weight("w1_2", t * P), here)
                    split_products(nc, ps[:, 1, :], weight("w2_2", t * P), here).then_inc(wide_done[t % 2], 1)
                values(b, 0)
                values(b, 1)
                u = 0
                for uses, name, n in ((USE_H1, "h1_2", 1), (USE_H2, "h2_2", 2)):
                    if n == 1:
                        pe.wait_ge(split, b * FT + FT + 1)
                    else:
                        was_read(pe, b, USE_H1[0])
                        was_read(pe, b, USE_H1[1])
                    for t in range(FT):
                        if t % 2 == 0:
                            ps = slot(b, uses[t // 2])
                        for kt in range(FT):
                            if n == 1:
                                last = split_products(nc, ps[:, t % 2, :], weight(name, kt * T + t * P),
                                                      (gate_high[:, kt, :], gate_low[:, kt, :]), kt == 0, kt == FT - 1)
                            else:
                                last = nc.tensor.matmul(ps[:, t % 2, :], w[name][:, kt * T + t * P:kt * T + (t + 1) * P],
                                                        hidden["h1_2"][:, kt, :], start=(kt == 0), stop=(kt == FT - 1))
                            for _ in range(int(t >= 2) if n == 1 else 2 * int(t < 2)):
                                if u == 0:
                                    pe.wait_ge(qq_ready, b * 4 + 4)
                                    pe.wait_ge(kk4_ready, b + 1)
                                    pe.wait_ge(lows_ready, b * 3 + 2)
                                    pe.wait_ge(o_read, b * H2 + 1)
                                maximum(b, u)
                                u += 1
                        if t % 2:
                            last.then_inc(wide_done[t // 2], 1)
                        if n == 2 and t == 1:
                            pe.wait_ge(max_read, b * H2 * NBLK + H2 * NBLK + 1)
                            pe.wait_ge(att_added, b)
                            nc.tensor.transpose(ps_o[0][0:H2 * NBLK, 1, 0:P], top[:, :, :].rearrange("p h m -> p (h m)"),
                                                ident).then_inc(maxT_done, 1)
                    if n == 1:
                        values(b, 2)
                        values(b, 3)
                        u += 8
                pe.wait_ge(pads, 1)
                pe.wait_ge(lows_ready, b * 3 + 3)
                pe.wait_ge(shifted, b * 16 + 16)
                scores(b, 0)
                was_read(pe, b, USE_H2[0])
                was_read(pe, b, USE_H2[1])
                for kt in range(FT):
                    last = nc.tensor.matmul(ps_o[0][:, 0, :], w["w3_2"][:, kt * P:(kt + 1) * P], hidden["h2_2"][:, kt, :],
                                            start=(kt == 0), stop=(kt == FT - 1))
                last.then_inc(y_done, 1)
                for h in range(H2):
                    if h + 1 < H2:
                        scores(b, h + 1)
                    was_read(pe, b, USE_S + 2 * h)
                    was_read(pe, b, USE_S + 2 * h + 1)
                    if h == 0:
                        pe.wait_ge(y_added, b + 1)
                    pe.wait_ge(o_read, b * H2 + h)
                    for n in range(NBLK):
                        out = ps_o[h % 2][:, n // 2, (n % 2) * (D + 1):(n % 2 + 1) * (D + 1)]
                        for m in range(NBLK):
                            last = nc.tensor.matmul(out, probs[:, (h + 1) % 2, m, n * P:(n + 1) * P], v[:, m, h, :],
                                                    start=(m == 0), stop=(m == NBLK - 1))
                    last.then_inc(o_done, 1)

            batch(0, None)
            with pe.Fori(1, B) as b:
                batch(b, b - 1)
            turn_attention(B - 1)


RING = 4
STARTS = ("la_rk", "la_vg", "la_d", "lb_d", "lb_r", "la_dd", "lb_k", "lb_dd", "lb_g", "lb_v", "r", "k", "g", "v")
ENDS = tuple(f"v_{j}" for j in range(HD3)) + ("u", "var")
BOTH = ("v_0", "v_1", "la_rk", "la_vg", "la_d", "v_2", "lb_d", "v_3", "lb_r", "v_4", "la_dd", "v_5", "lb_k", "v_6",
        "lb_dd", "lb_g", "v_7", "lb_v", "u", "r", "k", "var", "g", "v")
assert set(BOTH) == set(STARTS + ENDS) and len(BOTH) % RING == 0


class Turn:

    def __init__(self, b, a):
        self.b, self.a = b, a
        self.order = BOTH if a is not None and b is not None else STARTS if b is None else ENDS
        self.before = 0 if b is None else len(STARTS)
        self.turns = 0 if b is None else b * (len(BOTH) // RING)

    def bank(self, name):
        return (self.before + self.order.index(name)) % RING

    def earlier(self, name):
        return self.turns + (self.before + self.order.index(name)) // RING


FF_WEIGHTS = ("W1_3", "W2_3")


def layer3_mix(nc, sh):
    x, xn, w = sh["x"], sh["xn"], sh["w"][4]
    mean_all, mean_head = sh["common"]["mean_all"], sh["common"]["mean_head"]
    with ExitStack() as ctx:
        sb = lambda name, shape, dt=F32: ctx.enter_context(nc.sbuf_tensor(name, shape, dt))
        sem = lambda name: ctx.enter_context(nc.semaphore(name))
        zero = sb("zero3", [P, 1])
        dx, lerp = sb("dx3", [P, T]), sb("lerp3", [P, T])
        th = {n: sb(f"tanh_{n}", [P, T]) for n in ("rk", "vg", "d", "dd")}
        dmix = {n: sb(f"dmix_{n}", [P, T]) for n in "drkg"}
        xv = sb("xv3", [P, T])
        r, k, v, decay, ew = (sb(f"{n}3", [P, T]) for n in ("r", "k", "v", "decay", "log_decay"))
        tg, gate = sb("tg3", [P, T]), sb("gate3", [P, T])
        ruk = sb("ruk3", [P, T])
        kv = sb("kv3", [P, 2, T])
        st = sb("state3", [P, HD3, T])
        rs = sb("rs3", [P, 4, T])
        xv_high, xv_low = sb("xv_high3", [P, T]), sb("xv_low3", [P, T])
        first_v = w.part["vW"][0]
        vw = w.tensor[:, first_v:first_v + (1 + HD3) * P]
        vw_high, vw_low = sb("vw_high3", [P, (1 + HD3) * P]), sb("vw_low3", [P, (1 + HD3) * P])
        y, yc, sq, rstd, o = (sb(f"{n}3", [P, T]) for n in ("y", "yc", "sq", "rstd", "o"))
        hid = sb("hid3", [P, FT, T])
        mag, tern = ([sb(f"{name}3_{n}", [P, FF]) for n in range(2)] for name in ("mag", "tern"))
        row_sum = sb("row_sum3", [P, 2])
        bound = sb("bound3", [P, 6])
        ps_r = ctx.enter_context(nc.psum_tensor("ps_ring3", [P, RING, 512], F32))
        ps_f = ctx.enter_context(nc.psum_tensor("ps_f3", [P, 2, 512], F32))
        ps_y = ctx.enter_context(nc.psum_tensor("ps_y3", [P, 512], F32))
        ps_x = ctx.enter_context(nc.psum_tensor("ps_x3", [P, 512], F32))

        ring_done = [sem(f"ring_done{i}") for i in range(RING)]
        ring_read = [sem(f"ring_read{i}") for i in range(RING)]
        summed3, scaled = sem("summed3"), sem("scaled3")
        bound_ready = sem("bound_ready3")
        ternary = [sem("ternary3_0"), sem("ternary3_1")]
        dx_ready = sem("dx_ready")
        lerp_ready = sem("lerp_ready")
        xv_ready = sem("xv_ready")
        vw_high_ready, vw_ready = sem("vw_high_ready"), sem("vw_ready")
        ready = sem("ready3")
        tg_ready = sem("tg_ready")
        ruk_ready = sem("ruk_ready")
        scanned = sem("scanned3")
        rs_ready = sem("rs_ready")
        picked = sem("picked3")
        y_ready, y_mean, centred = sem("y_ready3"), sem("y_mean3"), sem("centred3")
        squared, rstd_ready, o_ready = sem("squared3"), sem("rstd_ready3"), sem("o_ready3")
        up_done, gelued = sem("up_done3"), sem("gelued3")
        out_done, x_added = sem("out_done3"), sem("x_added3")
        block = ctx.enter_context(nc.Block())

        def filled(eng, turn, name):
            bank = turn.bank(name)
            eng.wait_ge(ring_done[bank], turn.earlier(name) + 1)
            return ps_r[:, bank, :]

        def ternary_weight(nc_engine, eng, n):
            m = w[FF_WEIGHTS[n]]
            nc_engine.tensor_scalar(mag[n][:, :], m, bound[:, 4 + n:5 + n], None, ALU.is_lt)
            nc_engine.tensor_scalar(tern[n][:, :], m, bound[:, 2 + n:3 + n], None, ALU.is_gt)
            eng.drain()
            nc_engine.tensor_tensor(tern[n][:, :], tern[n][:, :], mag[n][:, :], ALU.subtract)
            eng.drain()
            nc_engine.tensor_tensor(tern[n][:, :], tern[n][:, :], m, ALU.subtract)
            eng.drain()
            nc_engine.tensor_tensor(m, m, tern[n][:, :], ALU.add).then_inc(ternary[n], 1)

        def turns(eng, turn_program, between=None):
            turn_program(Turn(None, 0))
            if between:
                between()
            with eng.Fori(0, B - 1) as b:
                turn_program(Turn(b, b + 1))
            turn_program(Turn(B - 1, None))

        @block.gpsimd
        def _(pool):
            nc.gpsimd.memset(zero[:, :], 0.0)
            pool.drain()
            pool.wait_ge(vw_high_ready, 1)
            nc.gpsimd.tensor_tensor(single(vw_low[:, :]), vw, vw_high[:, :], ALU.subtract).then_inc(vw_ready, 1)
            pool.drain()

            def turn_program(turn):
                a, b = turn.a, turn.b
                if a is not None:
                    pool.wait_ge(xv_ready, a)
                    nc.gpsimd.tensor_tensor(dx[:, 1:T], xn[:, bass.ds(a * T, T - 1)], xn[:, bass.ds(a * T + 1, T - 1)], ALU.subtract)
                    pool.drain()
                    nc.gpsimd.tensor_tensor(dx[:, 0:1], zero[:, :], xn[:, bass.ds(a * T, 1)], ALU.subtract).then_inc(dx_ready, 1)
                if b is not None:
                    for j in range(HD3):
                        pool.drain()
                        pool.wait_ge(picked, b * HD3 + j)
                        pool.wait_ge(scanned, b * HD3 + j + 1)
                        nc.gpsimd.tensor_tensor(rs[:, j % 4, :], r[:, :], st[:, j, :], ALU.mult).then_inc(rs_ready, 1)

            def make_ternary():
                pool.wait_ge(bound_ready, 1)
                ternary_weight(nc.gpsimd, pool, 1)
                pool.drain()

            turns(pool, turn_program, make_ternary)

        @block.scalar
        def _(act):
            act.wait_ge(sh["w_loaded"][4], 16)
            act.sem_inc(gelued, 1)

            def turn_program(turn):
                a, b = turn.a, turn.b
                read = lambda name: ring_read[turn.bank(name)]

                def tanh(name, to):
                    src = filled(act, turn, name)
                    nc.scalar.activation(to[:, :], src, ACT.Tanh).then_inc(read(name), 1)

                def gelu(t):
                    act.wait_ge(up_done, b * FT + t + 1)
                    nc.scalar.activation(hid[:, t, :], ps_f[:, t % 2, :], ACT.Gelu, bias=w["b1_3"][:, t:t + 1]).then_inc(gelued, 1)

                if a is not None:
                    tanh("la_rk", th["rk"])
                    tanh("la_vg", th["vg"])
                    tanh("la_d", th["d"])
                if b is not None:
                    gelu(0)
                    gelu(1)
                if a is not None:
                    tanh("la_dd", th["dd"])
                    src = filled(act, turn, "lb_dd")
                    nc.scalar.activation(ew[:, :], src, ACT.Exp, bias=w["ll_d"]).then_inc(read("lb_dd"), 1)
                if b is not None:
                    gelu(2)
                    gelu(3)
                if a is not None:
                    if b is not None:
                        act.wait_ge(rs_ready, b * HD3 + HD3)
                    for name, to in (("r", r), ("k", k)):
                        src = filled(act, turn, name)
                        nc.scalar.activation(to[:, :], src, ACT.Copy).then_inc(read(name), 1)
                if b is not None:
                    act.wait_ge(centred, b + 1)
                    nc.scalar.activation(sq[:, :], yc[:, :], ACT.Square).then_inc(squared, 1)
                if b is not None:
                    src = filled(act, turn, "var")
                    nc.scalar.activation(rstd[:, :], src, ACT.Ln, bias=sh["eps"][:, 0:1]).then_inc(read("var"), 1)
                    act.drain()
                    nc.scalar.activation(rstd[:, :], rstd[:, :], ACT.Exp, scale=-0.5).then_inc(rstd_ready, 1)
                if a is not None:
                    src = filled(act, turn, "g")
                    nc.scalar.activation(tg[:, :], src, ACT.Tanh, scale=0.5).then_inc(tg_ready, 1)
                if a is not None:
                    src = filled(act, turn, "v")
                    nc.scalar.activation(v[:, :], src, ACT.Copy).then_inc(read("v"), 1)
                    nc.scalar.activation(decay[:, :], ew[:, :], ACT.Exp, scale=-1.0).then_inc(ready, 1)

            turns(act, turn_program)

        @block.vector
        def _(dve):
            dve.wait_ge(sh["w_loaded"][4], 16)
            nc.vector.tensor_copy(single(vw_high[:, :]), vw).then_inc(vw_high_ready, 1)
            for n, name in enumerate(FF_WEIGHTS):
                nc.vector.scalar_tensor_tensor(mag[n][:, :], w[name], -1.0, w[name], ALU.mult, ALU.max)
                dve.drain()
                nc.vector.reduce_sum(row_sum[:, n:n + 1], mag[n][:, :], AX_X).then_inc(summed3, 1)
            dve.wait_ge(scaled, 1)
            nc.vector.tensor_scalar(bound[:, 0:2], ps_y[:, 0:2], 1.0 / FF, 1e-8, ALU.mult, ALU.max)
            dve.drain()
            nc.vector.tensor_scalar(bound[:, 2:4], bound[:, 0:2], 0.5, None, ALU.mult)
            nc.vector.tensor_scalar(bound[:, 4:6], bound[:, 0:2], -0.5, None, ALU.mult)
            dve.drain()
            dve.sem_inc(bound_ready, 1)
            nc.vector.tensor_copy(st[:, :, 0:1], w["state"].unsqueeze(2))

            def turn_program(turn):
                a, b = turn.a, turn.b
                read = lambda name: ring_read[turn.bank(name)]

                def scan(j):
                    if b is None:
                        return
                    src = filled(dve, turn, f"v_{j}")
                    nc.vector.tensor_tensor(kv[:, j % 2, :], k[:, :], src, ALU.mult).then_inc(read(f"v_{j}"), 1)
                    dve.drain()
                    nc.vector.tensor_tensor_scan(st[:, j, 1:T], decay[:, 0:T - 1], kv[:, j % 2, 0:T - 1], st[:, j, 0:1],
                                                 ALU.mult, ALU.add).then_inc(scanned, 1)

                def mix(name, to):
                    if a is None:
                        return
                    src = filled(dve, turn, f"lb_{name}")
                    nc.vector.scalar_tensor_tensor(to[:, :], src, w[f"ll_{name}"], dx[:, :],
                                                   ALU.add, ALU.mult).then_inc(read(f"lb_{name}"), 1)

                if b is not None:
                    dve.wait_ge(ready, b + 1)
                    nc.vector.scalar_tensor_tensor(ruk[:, :], r[:, :], w["u"], k[:, :], ALU.mult, ALU.mult).then_inc(ruk_ready, 1)
                if a is not None:
                    dve.wait_ge(dx_ready, a + 1)
                    nc.vector.scalar_tensor_tensor(lerp[:, :], dx[:, :], w["xw"], xn[:, at(a)], ALU.mult, ALU.add).then_inc(lerp_ready, 1)
                scan(0)
                scan(1)
                scan(2)
                mix("d", dmix["d"])
                scan(3)
                mix("r", dmix["r"])
                scan(4)
                scan(5)
                mix("k", dmix["k"])
                scan(6)
                mix("g", dmix["g"])
                scan(7)
                mix("v", xv)
                if a is not None:
                    dve.drain()
                    nc.vector.tensor_tensor(xv[:, :], xv[:, :], xn[:, at(a)], ALU.add)
                    dve.drain()
                    nc.vector.tensor_copy(single(xv_high[:, :]), xv[:, :])
                    dve.drain()
                    nc.vector.tensor_tensor(single(xv_low[:, :]), xv[:, :], xv_high[:, :], ALU.subtract).then_inc(xv_ready, 1)
                if b is not None:
                    src = filled(dve, turn, "u")
                    nc.vector.tensor_tensor(y[:, :], v[:, :], src, ALU.mult).then_inc(read("u"), 1)
                    dve.drain()
                    dve.wait_ge(picked, b * HD3 + HD3 + 3)
                    nc.vector.tensor_tensor(y[:, :], y[:, :], ps_y[:, :], ALU.add).then_inc(y_ready, 1)
                    dve.wait_ge(y_mean, b + 1)
                    nc.vector.tensor_tensor(yc[:, :], y[:, :], ps_y[:, :], ALU.subtract).then_inc(centred, 1)
                    dve.wait_ge(rstd_ready, b + 1)
                    nc.vector.tensor_tensor(o[:, :], yc[:, :], rstd[:, :], ALU.mult)
                    dve.drain()
                    nc.vector.tensor_scalar(o[:, :], o[:, :], w["ln_w"], w["ln_b"], ALU.mult, ALU.add)
                    dve.drain()
                    nc.vector.scalar_tensor_tensor(o[:, :], o[:, :], 0.5, gate[:, :], ALU.mult, ALU.mult).then_inc(o_ready, 1)
                if a is not None:
                    dve.drain()
                    dve.wait_ge(tg_ready, a + 1)
                    src = filled(dve, turn, "g")
                    nc.vector.scalar_tensor_tensor(gate[:, :], tg[:, :], 1.0, src, ALU.add, ALU.mult).then_inc(read("g"), 1)
                if b is not None:
                    dve.wait_ge(out_done, b + 1)
                    nc.vector.scalar_tensor_tensor(x[:, at(b)], ps_x[:, :], w["b2_3"], x[:, at(b)], ALU.add, ALU.add).then_inc(x_added, 1)

            def make_ternary():
                ternary_weight(nc.vector, dve, 0)

            turns(dve, turn_program, make_ternary)

        @block.tensor
        def _(pe):
            pe.sem_inc(picked, 3)
            pe.wait_ge(summed3, 2)
            nc.tensor.matmul(ps_y[:, 0:2], mean_all, row_sum[:, :], start=True, stop=True).then_inc(scaled, 1)
            pe.wait_ge(vw_ready, 1)

            def between():
                pe.wait_ge(bound_ready, 1)
                pe.wait_ge(ternary[0], 1)
                pe.wait_ge(ternary[1], 1)

            def turn_program(turn):
                a, b = turn.a, turn.b

                def v_product(name, part):
                    bank = turn.bank(name)
                    pe.wait_ge(ring_read[bank], turn.earlier(name))
                    cols = slice(part * P, (part + 1) * P)
                    split_products(nc, ps_r[:, bank, :], (vw_high[:, cols], vw_low[:, cols]),
                                   (xv_high[:, :], xv_low[:, :])).then_inc(ring_done[bank], 1)

                def product(name, *terms):
                    bank = turn.bank(name)
                    pe.wait_ge(ring_read[bank], turn.earlier(name))
                    for n, (lhsT, rhs) in enumerate(terms):
                        last = nc.tensor.matmul(ps_r[:, bank, :], w[lhsT] if isinstance(lhsT, str) else lhsT, rhs,
                                                start=(n == 0), stop=(n == len(terms) - 1))
                    last.then_inc(ring_done[bank], 1)

                def value(j):
                    if b is None:
                        return
                    if j == 0:
                        pe.wait_ge(xv_ready, b + 1)
                    v_product(f"v_{j}", 1 + j)

                def pick(j):
                    if b is None:
                        return
                    if j == 0:
                        pe.wait_ge(centred, b)
                    pe.wait_ge(rs_ready, b * HD3 + j + 1)
                    nc.tensor.matmul(ps_y[:, :], w["pick_j"][:, j * P:(j + 1) * P], rs[:, j % 4, :],
                                     start=(j == 0), stop=(j == HD3 - 1)).then_inc(picked, 1)

                def lora(name, of, tanh_of):
                    if a is None:
                        return
                    pe.wait_ge(ring_read[turn.bank(tanh_of)], turn.earlier(tanh_of) + 1)
                    product(name, (f"lb_{of}", th[tanh_of[3:]][:, :]))

                def written(of):
                    pe.wait_ge(ring_read[turn.bank(of)], turn.earlier(of) + 1)

                def up(t):
                    if b is None:
                        return
                    pe.wait_ge(gelued, b * FT + t)
                    nc.tensor.matmul(ps_f[:, t % 2, :], w["W1_3"][:, t * P:(t + 1) * P], xn[:, at(b)], start=True, stop=True).then_inc(up_done, 1)

                def down(t):
                    if b is None:
                        return
                    if t == 0:
                        pe.wait_ge(x_added, b)
                    pe.wait_ge(gelued, b * FT + t + 2)
                    nc.tensor.matmul(ps_x[:, :], w["W2_3"][:, t * P:(t + 1) * P], hid[:, t, :], start=(t == 0), stop=False)

                value(0)
                value(1)
                if a is not None:
                    pe.wait_ge(lerp_ready, a + 1)
                    for n in ("rk", "vg", "d"):
                        product(f"la_{n}", (f"la_{n}", lerp[:, :]))
                value(2)
                pick(0)
                up(0)
                up(1)
                lora("lb_d", "d", "la_d")
                value(3)
                pick(1)
                lora("lb_r", "r", "la_rk")
                value(4)
                pick(2)
                if a is not None:
                    written("lb_d")
                    product("la_dd", ("la_d", xn[:, at(a)]), ("la_d", dmix["d"][:, :]))
                value(5)
                pick(3)
                lora("lb_k", "k", "la_rk")
                value(6)
                pick(4)
                lora("lb_dd", "d", "la_dd")
                lora("lb_g", "g", "la_vg")
                value(7)
                pick(5)
                up(2)
                up(3)
                lora("lb_v", "v", "la_vg")
                pick(6)
                pick(7)
                if b is not None:
                    pe.wait_ge(ruk_ready, b + 1)
                    product("u", ("sum_head", ruk[:, :]))
                if a is not None:
                    for n in "rk":
                        written(f"lb_{n}")
                        product(n, (f"{n}W", xn[:, at(a)]), (f"{n}W", dmix[n][:, :]))
                if b is not None:
                    pe.wait_ge(y_ready, b + 1)
                    nc.tensor.matmul(ps_y[:, :], mean_head, y[:, :], start=True, stop=True).then_inc(y_mean, 1)
                down(0)
                down(1)
                if b is not None:
                    pe.wait_ge(squared, b + 1)
                    product("var", (mean_head, sq[:, :]))
                if a is not None:
                    written("lb_g")
                    product("g", ("gW", xn[:, at(a)]), ("gW", dmix["g"][:, :]))
                down(2)
                down(3)
                if a is not None:
                    pe.wait_ge(xv_ready, a + 1)
                    v_product("v", 0)
                if b is not None:
                    pe.wait_ge(o_ready, b + 1)
                    nc.tensor.matmul(ps_x[:, :], w["oW"], o[:, :], start=False, stop=True).then_inc(out_done, 1)

            turns(pe, turn_program, between)


def program(nc, x_dram, packs_dram, packs_width, out):
    with ExitStack() as top:
        sem = lambda name: top.enter_context(nc.semaphore(name))
        sb = lambda ctx, name, shape: ctx.enter_context(nc.sbuf_tensor(name, shape, F32))
        sh = {
            "x": sb(top, "x", [P, NTOK]), "xn": sb(top, "xn", [P, NTOK]), "eps": sb(top, "eps", [P, 2]),
            "x_dram": x_dram, "common_dram": packs_dram[0], "w_dram": packs_dram[1:], "w": {},
            "out": out,
            "cw_dram": nc.dram_tensor("combine_by_expert", (E0_TRUE, NTOK), F32, kind="Internal").ap(),
            "score_dram": nc.dram_tensor("score_by_expert", (E1, NTOK), F32, kind="Internal").ap(),
            "parts_dram": nc.dram_tensor("qk_parts", (2, 3, HD0, H0, T), BF16, kind="Internal").ap(),
            "x_loaded": [sem("x_loaded0"), sem("x_loaded1")], "common_loaded": sem("common_loaded"), "eps_set": sem("eps_set"),
            "scores_stored": sem("scores_stored"),
            "w_loaded": [sem(f"w_loaded{i}") for i in range(5)],
        }

        def pack(ctx, n):
            widths = packs_width[n]
            return Weights(sb(ctx, f"pack{n}", [P, sum(widths.values())]), widths)

        sh["common"] = pack(top, 0)
        with ExitStack() as ctx:
            sh["w"][0] = pack(ctx, 1)
            sh["logits0"] = ctx.enter_context(nc.sbuf_tensor("logits0", [P, NT, E0], F32))
            layer0_norm(nc, sh)
            layer0_mix(nc, sh)
        with ExitStack() as two:
            sh["w"][3] = pack(two, 4)
            for part in ("high", "low"):
                sh["w2_" + part] = Weights(sb(two, "w2_" + part, [P, sum(packs_width[3].values())]), packs_width[3])
            with ExitStack() as ctx:
                sh["w"][1] = pack(ctx, 2)
                sh["w"][2] = pack(ctx, 3)
                sh["score_rows"] = sb(ctx, "score_rows", [P, 2 * P])
                sh["decay"] = {n: sb(ctx, n, shape) for n, shape in (
                    ("lnd", [P, 1]), ("lnd_row", [P, DS]), ("d_o", [DS, C1]), ("d_v", [P, DS]), ("d_chunk", [P, DS]))}
                layer1_norm_and_route(nc, sh)
                layer1_mix(nc, sh)
            norm_only(nc, sh, "norm2")
            layer2_mix(nc, sh)
        with ExitStack() as ctx:
            sh["w"][4] = pack(ctx, 5)
            norm_only(nc, sh, "norm3", 4)
            layer3_mix(nc, sh)
        store_output(nc, sh)


def store_output(nc, sh):
    with ExitStack() as ctx:
        stored = ctx.enter_context(nc.semaphore("stored"))
        block = ctx.enter_context(nc.Block())

        @block.sync
        def _(sp):
            sp.dma_start(sh["out"], sh["x"][:, :]).then_inc(stored, 16)
            sp.wait_ge(stored, 16)


def kernel(**inputs):
    import concourse.bacc as bacc
    from concourse.bass_utils import run_bass_kernel_spmd

    nc = bacc.Bacc("TRN2", target_bir_lowering=False, num_devices=1)
    packs = packed(inputs)
    arrays = {"x": np.ascontiguousarray(np.asarray(inputs["L0_attn_x"]).reshape(NTOK, D).T)}
    for i, parts in enumerate(packs):
        arrays[f"pack{i}_dram"] = np.ascontiguousarray(np.concatenate(list(parts.values()), 1))
    widths = [{k: a.shape[1] for k, a in parts.items()} for parts in packs]
    dram = {n if n != "x" else "x_in": nc.dram_tensor(n if n != "x" else "x_in", a.shape, F32, kind="ExternalInput").ap()
            for n, a in arrays.items()}
    arrays["x_in"] = arrays.pop("x")
    out = nc.dram_tensor("out", (D, NTOK), F32, kind="ExternalOutput").ap()
    program(nc, dram["x_in"], [dram[f"pack{i}_dram"] for i in range(len(packs))], widths, out)
    result = run_bass_kernel_spmd(nc, [arrays], core_ids=[0]).results[0]["out"]
    return np.ascontiguousarray(result.T).reshape(B, T, D)
```
